# Optimizing a Trainium2 kernel written in Bass

```python
import numpy as np
import jax
import jax.numpy as jnp

def _softmax(x, axis=-1):
    return jax.nn.softmax(x, axis=axis)

def _gelu(x):
    return jax.nn.gelu(x, approximate=True)

def _silu(x):
    return jax.nn.silu(x)

def _sigmoid(x):
    return jax.nn.sigmoid(x)

def _layernorm(x, axis=-1, eps=1e-05):
    m = jnp.mean(x, axis=axis, keepdims=True)
    v = jnp.var(x, axis=axis, keepdims=True)
    return (x - m) / jnp.sqrt(v + eps)

def _scatter_add(tgt, idx, src, axis=0):
    return tgt.at[idx].add(src)

def _segment_sum(src, seg, n):
    return jax.ops.segment_sum(src, seg, n)
kernel_name = 'mk_gnn_resnorm_d2_gnn_r8_e627a1'

def setup_inputs(seed: int=0):
    np.random.seed(seed)
    _w = jnp.asarray

    def _rec_inputs():
        import jax
        import jax.numpy as jnp
        _gk = jax.random.key(seed)
        x = -0.0001079 + 1 * jax.random.normal(jax.random.fold_in(_gk, 1), (6250, 64), jnp.float32)
        _s = jax.random.randint(jax.random.fold_in(_gk, 2), (100000,), 0, 6250, jnp.int32)
        _d = jax.random.randint(jax.random.fold_in(_gk, 3), (100000,), 0, 6250, jnp.int32)
        _loop = jnp.arange(6250, dtype=jnp.int32)
        src = jnp.concatenate([_s, _d, _loop])
        dst = jnp.concatenate([_d, _s, _loop])
        _o = jnp.argsort(dst, stable=True)
        src = src[_o]
        dst = dst[_o]
        edge_attr_64 = -8.16379e-05 + 0.999858 * jax.random.normal(jax.random.fold_in(_gk, 12), (206250, 64), jnp.float32)
        edge_type_4 = jax.random.randint(jax.random.fold_in(_gk, 14), (206250,), 0, 4, jnp.int32)
        return (x, src, dst, edge_attr_64, edge_type_4)
    x, src, dst, edge_attr_64, edge_type_4 = _rec_inputs()

    def _L0_gnn_setup():
        import jax, jax.numpy as jnp
        import numpy as np
        NEG_SLOPE = 0.2
        key = jax.random.key(seed)
        ks = jax.random.split(key, 10)
        N, E, D = (6250, 156250, 64)
        indices = jax.random.randint(ks[0], (2, E), 0, N, dtype=jnp.int64)
        features = jax.random.normal(ks[1], (N, D), dtype=jnp.float32)
        edge_types = jax.random.randint(ks[2], (E,), 0, 4, dtype=jnp.int64)
        s = 1.0 / np.sqrt(D)
        return {'indices': indices, 'features': features, 'edge_types': edge_types, 'num_nodes': N, 'W1_w': jax.random.uniform(ks[3], (D, D), jnp.float32, -s, s), 'W1_b': jax.random.uniform(ks[4], (D,), jnp.float32, -s, s), 'W2_w': jax.random.uniform(ks[5], (D, D), jnp.float32, -s, s), 'W2_b': jax.random.uniform(ks[6], (D,), jnp.float32, -s, s), 'W_att_w': jax.random.uniform(ks[7], (D, D), jnp.float32, -s, s), 'W_att_b': jax.random.uniform(ks[8], (D,), jnp.float32, -s, s), 'a': jax.random.normal(ks[9], (2 * D, 1), jnp.float32) * np.sqrt(2.0 / (2 * D + 1))}
    _L0_gnn_all = _L0_gnn_setup()
    _L0_gnn_in = {k: v for k, v in _L0_gnn_all.items() if k in ('W1_w', 'W1_b', 'W2_w', 'W2_b', 'W_att_w', 'W_att_b', 'a')}
    del _L0_gnn_all

    def _L1_gnn_setup():
        import jax, jax.numpy as jnp
        import numpy as np
        N_NODES = 12500

        def _segment_softmax(e, dst, num_segments):
            m = jax.ops.segment_max(e, dst, num_segments=num_segments)
            m = jnp.where(jnp.isfinite(m), m, 0.0)
            ex = jnp.exp(e - m[dst])
            denom = jax.ops.segment_sum(ex, dst, num_segments=num_segments)
            return ex / denom[dst]
        key = jax.random.key(seed)
        ks = jax.random.split(key, 8)
        N, E, Din, Dout = (N_NODES, 200000, 64, 64)
        node_h = jax.random.normal(ks[0], (N, Din), jnp.float32)
        edge_h = jax.random.normal(ks[1], (E, Din), jnp.float32)
        src = jax.random.randint(ks[2], (E,), 0, N, dtype=jnp.int32)
        dst = jax.random.randint(ks[3], (E,), 0, N, dtype=jnp.int32)
        s = float(np.sqrt(2.0 / (Din + Dout)))
        W_fc = jax.random.normal(ks[4], (Dout, Din), jnp.float32) * s
        W_fcr = jax.random.normal(ks[5], (Dout, Din), jnp.float32) * s
        loop_W = jax.random.normal(ks[6], (Dout, Dout), jnp.float32) * s
        return {'node_h': node_h, 'edge_h': edge_h, 'src': src, 'dst': dst, 'W_fc': W_fc, 'W_fcr': W_fcr, 'loop_W': loop_W}
    _L1_gnn_all = _L1_gnn_setup()
    _L1_gnn_in = {k: v for k, v in _L1_gnn_all.items() if k in ('W_fc', 'W_fcr', 'loop_W')}
    del _L1_gnn_all
    return {'x': x, 'src': src, 'dst': dst, 'edge_attr_64': edge_attr_64, 'edge_type_4': edge_type_4, 'L0_gnn_W1_w': _L0_gnn_in['W1_w'], 'L0_gnn_W1_b': _L0_gnn_in['W1_b'], 'L0_gnn_W2_w': _L0_gnn_in['W2_w'], 'L0_gnn_W2_b': _L0_gnn_in['W2_b'], 'L0_gnn_W_att_w': _L0_gnn_in['W_att_w'], 'L0_gnn_W_att_b': _L0_gnn_in['W_att_b'], 'L0_gnn_a': _L0_gnn_in['a'], 'L1_gnn_W_fc': _L1_gnn_in['W_fc'], 'L1_gnn_W_fcr': _L1_gnn_in['W_fcr'], 'L1_gnn_loop_W': _L1_gnn_in['loop_W']}

def reference(x, src, dst, edge_attr_64, edge_type_4, L0_gnn_W1_w, L0_gnn_W1_b, L0_gnn_W2_w, L0_gnn_W2_b, L0_gnn_W_att_w, L0_gnn_W_att_b, L0_gnn_a, L1_gnn_W_fc, L1_gnn_W_fcr, L1_gnn_loop_W):
    import jax
    import jax.numpy as jnp

    def _L0_gnn_ref(indices, features, edge_types, num_nodes, W1_w, W1_b, W2_w, W2_b, W_att_w, W_att_b, a):
        import jax, jax.numpy as jnp
        import numpy as np
        NEG_SLOPE = 0.2
        src, dst = (indices[0], indices[1])
        D = W_att_w.shape[0]
        scaling = 1.0 / jnp.sqrt(jnp.float32(D))
        h_trans = features @ W_att_w.T + W_att_b
        a1, a2 = (a[:D, 0], a[D:, 0])
        s_src = h_trans @ a1
        s_dst = h_trans @ a2
        e_raw = s_src[src] + s_dst[dst]
        bias = jnp.where(edge_types == 0, 5.0, 0.0)
        e = jax.nn.leaky_relu((e_raw + bias) * scaling, NEG_SLOPE).astype(jnp.float32)
        max_score = jax.lax.stop_gradient(jax.ops.segment_max(e, dst, num_segments=num_nodes))
        max_score = jnp.where(jnp.isfinite(max_score), max_score, -1000000000.0)
        exp_e = jnp.exp(e - max_score[dst])
        denom = jax.ops.segment_sum(exp_e, dst, num_segments=num_nodes)
        alpha = exp_e / (denom[dst] + 1e-09)
        h_msg = features @ W1_w.T + W1_b
        weighted = h_msg[src] * alpha[:, None]
        h_neigh = jax.ops.segment_sum(weighted, dst, num_segments=num_nodes)
        h_self = features
        sum_h = h_self + h_neigh
        prod_h = h_self * h_neigh
        h_out = jax.nn.leaky_relu(sum_h + prod_h @ W2_w.T + W2_b, NEG_SLOPE)
        return h_out

    def _L1_gnn_ref(node_h, edge_h, src, dst, W_fc, W_fcr, loop_W):
        import jax, jax.numpy as jnp
        import numpy as np
        N_NODES = 12500

        def _segment_softmax(e, dst, num_segments):
            m = jax.ops.segment_max(e, dst, num_segments=num_segments)
            m = jnp.where(jnp.isfinite(m), m, 0.0)
            ex = jnp.exp(e - m[dst])
            denom = jax.ops.segment_sum(ex, dst, num_segments=num_segments)
            return ex / denom[dst]
        N = node_h.shape[0]
        h = node_h @ W_fc.T
        eh = edge_h @ W_fcr.T
        alpha = _segment_softmax(eh, dst, N)
        z = h[src]
        agg = jax.ops.segment_sum(alpha * (z + eh), dst, num_segments=N)
        deg = jax.ops.segment_sum(jnp.ones((dst.shape[0],), h.dtype), dst, num_segments=N)
        h_new = jnp.where((deg > 0)[:, None], agg + h @ loop_W, h)
        return jax.nn.relu(h_new)
    edge_index = jnp.stack([src, dst])
    x = _layernorm(x + _L0_gnn_ref(edge_index, x, edge_type_4, 6250, L0_gnn_W1_w, L0_gnn_W1_b, L0_gnn_W2_w, L0_gnn_W2_b, L0_gnn_W_att_w, L0_gnn_W_att_b, L0_gnn_a), axis=-1)
    x = _layernorm(x + _L1_gnn_ref(x, edge_attr_64, src, dst, L1_gnn_W_fc, L1_gnn_W_fcr, L1_gnn_loop_W), axis=-1)
    return x

_drawn_inputs = setup_inputs


def setup_inputs(seed=0):
    import zlib

    import numpy as np

    out = dict(_drawn_inputs(seed))
    spreads = {}
    factors = {'L0_gnn_W_att_w': 8.0, 'L0_gnn_W_att_b': 22.995, 'L0_gnn_a': 8.0}
    for name, (base, spread) in spreads.items():
        noise = np.random.default_rng([zlib.crc32(name.encode()), seed]).standard_normal(out[name].shape)
        drawn = base * np.exp(spread * noise) if base else spread * noise
        out[name] = jnp.asarray(drawn.astype(out[name].dtype))
    for name, factor in factors.items():
        out[name] = (out[name] * factor).astype(out[name].dtype)
    return out
```

```python
import concourse.bass as bass
from concourse import mybir
from contextlib import ExitStack

P = 128
D = 64
N = 6250
E = 206250
TPC = 4
CH = TPC * P
NCH = -(-E // (2 * CH))
HT = NCH * TPC
HALF = HT * P
T = 2 * HT
SPC = 2 * TPC
NT = -(-N // P)
NPAD = NT * P
ACCW = NPAD + P
GT = 7
NG = NT // GT
XW = D + 2
BIG = float(2.0 ** 100)
NW = 32
META = 12
UNROLL = 4
HEAD = 2 * UNROLL
BLK = -(-T // P)


def lagged(m, u, lag):
    d = u - lag
    return m * UNROLL + d, d % 4, m + d // 4, d % 2, m * 2 + d // 2


def live(m, k):
    return not isinstance(m, int) or 0 <= k < NCH


def late(m, count):
    return not isinstance(m, int) or count > 0


def run_steps(eng, lags, step):
    total = NCH + lags
    loops = (NCH - HEAD) // UNROLL
    for s in range(HEAD):
        step(s // UNROLL, s % UNROLL)
    with eng.Fori(HEAD // UNROLL, HEAD // UNROLL + loops) as m:
        for u in range(UNROLL):
            step(m, u)
    for s in range(HEAD + loops * UNROLL, total):
        step(s // UNROLL, s % UNROLL)


def edge_loads(m, k):
    if not isinstance(m, int):
        return 2
    left = min(max(E - HALF - k * CH, 0), CH)
    return 1 + (left >= P) + (left % P > 0)


assert HEAD + (NCH - HEAD) // UNROLL * UNROLL <= (E - HALF) // CH


class Chain:

    def __init__(self, eng, sem, base=0):
        self.eng, self.sem, self.base, self.n = eng, sem, base, 0

    def __call__(self, ins):
        ins.then_inc(self.sem, 1)
        self.n += 1
        self.eng.wait_ge(self.sem, self.base + self.n)


def gnn_kernel(nc, x, src, dst, edge_attr, edge_type, W1, b1, W2, b2, Watt, batt, a, Wfc, Wfcr, loopW, out):
    f32, i32, u32, bf16 = mybir.dt.float32, mybir.dt.int32, mybir.dt.uint32, mybir.dt.bfloat16
    ALU, ACT, AX = mybir.AluOpType, mybir.ActivationFunctionType, mybir.AxisListType
    ds = bass.ds

    xtab = nc.dram_tensor("xtab", (NPAD, XW), f32).ap()
    htab = nc.dram_tensor("htab", (NPAD, D), f32).ap()
    negd = nc.dram_tensor("negd", (2 * HALF,), bf16).ap()

    ctx = ExitStack()
    with ctx:
        def sb(name, shape, dt=f32):
            return ctx.enter_context(nc.sbuf_tensor(name, shape, dt))

        def sem(name):
            return ctx.enter_context(nc.semaphore(name))

        srcT = sb("srcT", [P, T], u32)
        relT = sb("relT", [P, T])
        biasT = sb("biasT", [P, T])
        relC = sb("relC", [P, T])
        meta = sb("meta", [1, NCH * META], i32)
        bnd = sb("bnd", [P, NCH])
        acc = [sb("accA", [P, ACCW]), sb("accB", [P, ACCW])]
        xs = sb("xs", [P, NT, D])
        hh = sb("hh", [P, 2, NT * D])
        hs = hh[:, 0, :].rearrange("p (t c) -> p t c", c=D)
        hl = hh[:, 1, :].rearrange("p (t c) -> p t c", c=D)
        xtb = hh[:, :, :].rearrange("p a b -> p (a b)")[:, 0:NT * XW].rearrange("p (t c) -> p t c", c=XW)
        xT = acc[0]
        ident = sb("ident", [P, P])
        pick = sb("pick", [P, 2, P])
        iota = sb("iota", [P, P])
        iota_i = sb("iota_i", [P, P], i32)
        ones = sb("ones", [1, P])
        W1b = sb("W1b", [D + 1, D + 1])
        W2b = sb("W2b", [D + 1, D])
        WfcT = sb("WfcT", [D, D])
        loopS = sb("loopS", [D, D])
        BD = sb("BD", [P, P])
        vc = sb("vc", [D + 1, 2])
        wl = sb("wl", [D, 5 * D + D + 1 + 2])
        wW1, wW2, wWfc = (wl[:, i * D:(i + 1) * D] for i in range(3))
        wWfcr = wl[:, 3 * D:5 * D]
        wAtt = wl[:, 5 * D:6 * D + 1]
        wa = wl[:, 6 * D + 1:6 * D + 3]
        bndM = sb("bndM", [P, 2])
        cont = sb("cont", [P, 1], bf16)
        join = sb("join", [P, 8])

        NF = 10752
        arena = sb("arena", [P, NF])
        at = [0]

        def carve(n, dt=f32):
            w = n if dt in (f32, i32, u32) else -(-n // 2)
            ap = arena[:, at[0]:at[0] + w]
            at[0] += w
            assert at[0] <= NF
            return ap if dt == f32 else ap.bitcast(dt)

        ixb = [sb(f"ixb{i}", [P, SPC], u32) for i in range(4)]
        relb = [sb(f"relb{i}", [P, SPC]) for i in range(4)]
        relc = [sb(f"relc{i}", [P, SPC]) for i in range(4)]
        z = [carve(SPC * XW) for _ in range(4)]
        z0 = [t.rearrange("p (s c) -> p s c", c=XW) for t in z]
        z1 = [t[:, 0:SPC * D].rearrange("p (s c) -> p s c", c=D) for t in z]
        neg = [sb(f"neg{i}", [P, CH + 1], bf16) for i in range(2)]
        F = [carve(CH) for _ in range(2)]
        M = [carve(CH) for _ in range(2)]
        oh = [carve(SPC * P).rearrange("p (s w) -> p s w", w=P) for _ in range(2)]
        drop = sb("drop", [P, 2])
        fac = sb("fac", [P, 4])
        ub = sb("ub", [P, 2 * SPC])
        us = sb("us", [P, 2 * SPC])
        ubb = sb("ubb", [P, 2 * SPC])
        ts = sb("ts", [P, 2 * SPC])
        es = sb("es", [P, 2 * SPC])
        pd = sb("pd", [P, 2 * SPC])
        pe_ = sb("pe_", [P, 2 * SPC])
        junk = carve(SPC * NW)
        ohn = [carve(SPC * NW).rearrange("p (s w) -> p s w", w=NW) for _ in range(4)]
        eb = carve(CH)
        merged = carve(GT * P)
        rden = sb("rden", [P, GT * D])
        n1, n2, n3, n4 = (carve(GT * D) for _ in range(4))
        mean = sb("mean", [P, 4 * GT])
        prodT = sb("prodT", [D + 1, GT * P])
        hT = sb("hT", [D, GT * P])
        big = sb("big", [P, ACCW])
        sdst = big
        at1 = [0]

        def carve1(n):
            ap = big[:, at1[0]:at1[0] + n]
            at1[0] += n
            assert at1[0] <= ACCW
            return ap

        ed = [carve1(CH) for _ in range(2)]
        edT = [carve1(CH) for _ in range(2)]
        Xs = carve1(CH)
        Ex = [carve1(CH) for _ in range(2)]
        Y = carve1(CH)
        V = [carve1(SPC * P).rearrange("p (s c) -> p s c", c=P) for _ in range(2)]
        assert at1[0] <= ACCW
        at[0] = 0
        reach2 = carve(2 * NCH)[0:1, :].rearrange("p (h k) -> p h k", h=2)
        drow = carve(HT * 2 + 1, i32)
        negs = carve(HT * 2, bf16)
        rows = carve(BLK * P, i32).rearrange("p (b j) -> p b j", j=P)
        rowf = carve(BLK * P).rearrange("p (b j) -> p b j", j=P)
        dT = carve(T)

        ps = ctx.enter_context(nc.psum_tensor("ps", [P, 8 * 512], f32))

        def bank(i, a=0, b=512):
            return ps[:, i * 512 + a:i * 512 + b]

        s_const = sem("const_ready")
        s_w = sem("weights_loaded")
        s_x = sem("x_loaded")
        s_drow = sem("dst_flat_loaded")
        s_pads = sem("pads_set")
        s_rows = sem("rows_loaded")
        s_rowf = sem("rows_converted")
        s_rowT = sem("rows_transposed")
        s_tab = sem("table_written")
        s_negs = sem("flags_ready")
        s_negd = sem("flags_stored")
        s_cont = sem("cont_loaded")
        s_bc = sem("bases_broadcast")
        s_wT = sem("weights_transposed")
        s_wS = sem("weights_ready")
        s_xT = sem("x_transposed")
        s_xTs = sem("xT_ready")
        s_sps = sem("node_scores")
        s_sd = sem("sdst_product")
        s_sds = sem("sdst_ready")
        s_xtb = sem("xtab_built")
        s_xtd = sem("xtab_stored")
        s_dve = sem("dve_chain")
        s_act = sem("act_chain")
        layers = []
        for L in range(2):
            layers.append({n: sem(f"{n}{L}") for n in (
                "neg_loaded_0", "neg_loaded_1", "ix_ready", "rel_ready",
                "z_loaded_0", "z_loaded_1", "z_loaded_2", "z_loaded_3",
                "fwd_done", "max_done", "drop_ready", "bnd_done", "fac_product", "fac_ready",
                "onehot_ready", "sum_done", "acc_done", "zero_done",
                "merged", "n_product", "xn_ready", "prodT", "prodTs", "w2_product", "x1_ready",
                "x1T", "x1Ts", "h_product", "h_ready", "hT_ready", "hl_product", "h_stored",
                "dve_epi", "var_ready", "std_ready", "join_product", "join_ready", "join_exp", "layer_done")})
        s_u = sem("u_ready")
        s_e = sem("e_ready")
        s_eb = sem("e_spread")
        s_et = sem("eT_ready")
        s_mt = sem("maxT_ready")
        s_pd = sem("pd_ready")
        s_p = sem("p_ready")
        s_t = sem("t_done")
        s_ed = [sem("edge_loaded_0"), sem("edge_loaded_1")]
        s_edT = sem("edgeT_product")
        s_edTs = sem("edgeT_ready")
        s_eh = sem("ehT_ready")
        s_ehe = sem("eh_ready")
        s_xsub = sem("x_sub")
        s_ex = sem("ex_ready")
        s_exT = sem("exT_product")
        s_den = sem("den_ready")
        s_y = sem("y_ready")
        s_val = sem("values_ready")
        s_out = sem("out_stored")

        NCONST = 14

        s_apart = sem("apart")

        def apart(eng):
            eng.sem_inc(s_apart, 1)

        block = ctx.enter_context(nc.Block())

        def chunk_meta(eng, k, count):
            _, got = nc.values_load_multi_w_load_instructions(
                meta[0:1, ds(k * META, count)], engines=[eng.engine], min_val=0, max_val=N,
                skip_runtime_bounds_check_because="dst values, N for padding, or a difference of two")
            return got

        def table(t, k, step=1):
            return t[:, ds(k * SPC, SPC)]

        @block.sync
        def _(sp):
            for view, w in ((wW1, W1), (wW2, W2), (wWfc, Wfc), (wWfcr[:, 0:D], Wfcr), (wWfcr[:, D:2 * D], Wfcr),
                            (wAtt[:, 0:D], Watt)):
                sp.dma_start(view, w).then_inc(s_w, 16)
            sp.dma_start(wAtt[:, D:D + 1], batt.rearrange("(o i) -> o i", i=1)).then_inc(s_w, 16)
            sp.dma_start(wa[:, 0:1], a[0:D, :]).then_inc(s_w, 16)
            sp.dma_start(wa[:, 1:2], a[D:2 * D, :]).then_inc(s_w, 16)
            sp.dma_start(loopS[:, :], loopW).then_inc(s_w, 16)
            sp.wait_ge(s_const, 1)
            full = (NT - 1) * P
            sp.dma_start(xs[:, 0:NT - 1, :], x[0:full, :].rearrange("(t p) c -> p t c", p=P)).then_inc(s_x, 16)
            sp.dma_start(xs[0:N - full, NT - 1, :], x[full:N, :]).then_inc(s_x, 16)
            sp.wait_ge(s_const, 3)
            sp.dma_start(W1b[D:D + 1, 0:D], b1.rearrange("(i o) -> i o", i=1)).then_inc(s_w, 16)
            sp.dma_start(W2b[D:D + 1, :], b2.rearrange("(i o) -> i o", i=1)).then_inc(s_w, 16)
            sp.wait_ge(s_const, 5)
            EP = T
            full = E // EP
            for lo, hi in ((0, full // 16 * 16), (full // 16 * 16, full)):
                sp.dma_start(drow[lo:hi, 1:EP + 1],
                             dst[lo * EP:hi * EP].rearrange("(p e) -> p e", e=EP)).then_inc(s_drow, 16)
            sp.dma_start(drow[full:full + 1, 1:E - full * EP + 1],
                         dst[full * EP:E].rearrange("(p e) -> p e", p=1)).then_inc(s_drow, 16)
            last = dst[0:(P - 1) * EP].rearrange("(p e) -> p e", e=EP)[:, EP - 1:EP]
            with nc.allow_non_contiguous_dma(reason="one element per partition"):
                sp.dma_start(drow[1:113, 0:1], last[0:112, :]).then_inc(s_drow, 16)
                sp.dma_start(drow[113:P, 0:1], last[112:P - 1, :]).then_inc(s_drow, 16)
            for n, arr in enumerate((dst, edge_type, src)):
                sp.wait_ge(s_pads, n + 1)
                whole = E // P // P * P
                nb = whole // P
                sp.dma_start(rows[:, 0:nb, :], arr[0:whole * P].rearrange("(b q j) -> q b j", q=P, j=P)).then_inc(s_rows, 16)
                rest = E // P - whole
                sp.dma_start(rows[0:rest, nb, :],
                             arr[whole * P:(whole + rest) * P].rearrange("(q j) -> q j", j=P)).then_inc(s_rows, 16)
                sp.dma_start(rows[rest:rest + 1, nb, 0:E % P],
                             arr[(whole + rest) * P:E].rearrange("(q j) -> q j", q=1)).then_inc(s_rows, 16)
            sp.wait_ge(s_negs, 1)
            sp.dma_start(negd.rearrange("(p e) -> p e", p=P), negs).then_inc(s_negd, 16)
            sp.wait_ge(s_xtb, 1)
            sp.dma_start(xtab.rearrange("(t p) c -> p t c", p=P), xtb).then_inc(s_xtd, 16)
            sp.wait_ge(s_negd, 16)
            sp.dma_start(cont[:, :], negd[HALF:HALF + 1].rearrange("(a b) -> a b", b=1).to_broadcast([P, 1])).then_inc(s_cont, 16)

            def load_flags(L, m, u):
                k, _, _, s2, n2 = lagged(m, u, 0)
                if live(m, k):
                    if late(m, n2):
                        sp.wait_ge(L["max_done"], k - 1)
                    for h in range(2):
                        part = negd[ds(h * HALF + k * CH, CH)].rearrange("(a e) -> a e", a=1)
                        sp.dma_start(neg[s2][h * D:(h + 1) * D, 0:CH], part.to_broadcast([D, CH])).then_inc(L[f"neg_loaded_{s2}"], 16)

            run_steps(sp, 0, lambda m, u: load_flags(layers[0], m, u))

            with sp.Fori(0, NG) as g:
                sp.wait_ge(layers[0]["h_ready"], g + 1)
                sp.dma_start(htab[ds(g * (GT * P), GT * P), :].rearrange("(t p) c -> p t c", p=P),
                             hs[:, ds(g * GT, GT), :]).then_inc(layers[0]["h_stored"], 16)

            def load_edges(m, u):
                load_flags(layers[1], m, u)
                k, _, _, s2, n2 = lagged(m, u, 0)
                if live(m, k):
                    if late(m, n2):
                        sp.wait_ge(s_edT, k - 1)
                    by_half = ed[s2].rearrange("p (i h c) -> p i h c", i=TPC, h=2)
                    for h in range(2):
                        left = E - HALF - k * CH if h and isinstance(m, int) else CH
                        whole, rest = min(max(left, 0), CH) // P, min(max(left, 0), CH) % P
                        if whole:
                            sp.dma_start(by_half[:, 0:whole, h, :], edge_attr[ds(h * HALF + k * CH, whole * P), :].rearrange(
                                "(i p) c -> p i c", p=P)).then_inc(s_ed[s2], 16)
                        if rest:
                            sp.dma_start(by_half[0:rest, whole, h, :], edge_attr[E - rest:E, :]).then_inc(s_ed[s2], 16)

            sp.wait_ge(layers[0]["layer_done"], 1)
            run_steps(sp, 0, load_edges)

            full = NT - 1
            sp.wait_ge(layers[1]["layer_done"], 1)
            sp.dma_start(out[0:full * P, :].rearrange("(t p) c -> p t c", p=P), hs[:, 0:full, :]).then_inc(s_out, 16)
            sp.dma_start(out[full * P:N, :], hs[0:N - full * P, full, :]).then_inc(s_out, 16)
            sp.wait_ge(s_out, 32)

        @block.gpsimd
        def _(g):
            g.memset(xs[:, NT - 1, :], 0.0).then_inc(s_const, 1)
            g.memset(W1b[:, :], 0.0).then_inc(s_const, 1)
            g.memset(W2b[:, :], 0.0).then_inc(s_const, 1)
            g.memset(drow, N).then_inc(s_const, 1)
            g.wait_ge(s_const, 4)
            g.memset(drow[0:1, 0:1], -1).then_inc(s_const, 1)
            g.memset(ident[:, :], 0.0).then_inc(s_const, 1)
            g.wait_ge(s_const, 6)
            g.affine_select(out=ident[:, :], in_=ident[:, :], compare_op=ALU.not_equal, fill=1.0,
                            base=0, pattern=[[-1, P]], channel_multiplier=1).then_inc(s_const, 1)
            g.iota(iota_i[:, :], pattern=[[1, P]], base=0, channel_multiplier=0).then_inc(s_const, 1)
            for t, value in ((ones[:, :], 1.0), (BD[:, :], 0.0), (bndM[:, :], -BIG), (neg[0][:, CH:CH + 1], 0.0),
                             (neg[1][:, CH:CH + 1], 0.0), (acc[1][:, :], 0.0)):
                g.memset(t, value).then_inc(s_const, 1)

            def gather(L, tab, zz, m, u):
                k, s4, n4, _, _ = lagged(m, u, 0)
                if not live(m, k):
                    return
                g.wait_ge(L["ix_ready"], k + 1)
                if late(m, n4):
                    g.wait_ge(L["sum_done"] if zz is z0 else s_y, k - 3)
                apart(g)
                for s in range(SPC):
                    w = XW if zz is z0 else D
                    g.indirect_dma_start(zz[s4][:, s, 0:w], None, tab[:, :],
                                         bass.IndirectOffsetOnAxis(ap=ixb[s4][:, s:s + 1], axis=0)
                                         ).then_inc(L[f"z_loaded_{s4}"], 16)

            g.wait_ge(s_xtd, 16)
            run_steps(g, 0, lambda m, u: gather(layers[0], xtab, z0, m, u))
            g.wait_ge(layers[0]["h_stored"], 16 * NG)
            run_steps(g, 0, lambda m, u: gather(layers[1], htab, z1, m, u))

        @block.scalar
        def _(act):
            chain = Chain(act, s_act)
            for q in range(-(-NPAD // 512)):
                w = min(512, NPAD - q * 512)
                act.wait_ge(s_xT, q + 1)
                act.activation(xT[0:D, q * 512:q * 512 + w], bank(4 + q % 4, 0, w)[0:D, :], ACT.Copy).then_inc(s_xTs, 1)
            for q in range(-(-NPAD // 512)):
                w = min(512, NPAD - q * 512)
                act.wait_ge(s_sd, q + 1)
                act.activation(sdst[:, q * 512:q * 512 + w], bank(4 + q % 2, 0, w), ACT.Copy, scale=0.125).then_inc(s_sds, 1)

            def copy_params(L, m, u):
                k, s4, n4, _, _ = lagged(m, u, 0)
                if live(m, k):
                    if late(m, n4):
                        act.wait_ge(L[f"z_loaded_{s4}"], n4 * (16 * SPC))
                        act.wait_ge(L["onehot_ready"], (k - 3) * SPC)
                    act.activation(ixb[s4][:, :], table(srcT, k), ACT.Copy).then_inc(L["ix_ready"], 1)
                    act.activation(relb[s4][:, :], table(relT, k), ACT.Copy).then_inc(L["rel_ready"], 1)
                    act.activation(relc[s4][:, :], table(relC, k), ACT.Copy).then_inc(L["rel_ready"], 1)

            def exp_fac(L, m, u, lag):
                k, _, _, s2, n2 = lagged(m, u, lag)
                if live(m, k):
                    act.wait_ge(L["fac_product"], k + 1)
                    if late(m, n2):
                        act.wait_ge(L["acc_done"], (k - 1) * SPC)
                    act.activation(fac[:, 2 * s2:2 * s2 + 2], bank(7, 0, 2), ACT.Exp,
                                   scale=-1.0).then_inc(L["fac_ready"], 1)

            def step0(m, u):
                L = layers[0]
                copy_params(L, m, u)
                k, _, _, s2, n2 = lagged(m, u, 3)
                if live(m, k):
                    act.wait_ge(s_pd, k + 1)
                    if late(m, n2):
                        act.wait_ge(L["onehot_ready"], (k - 1) * SPC)
                    act.activation(pe_[:, s2 * SPC:(s2 + 1) * SPC], pd[:, s2 * SPC:(s2 + 1) * SPC], ACT.Exp).then_inc(s_p, 1)
                exp_fac(L, m, u, 3)
                k, _, _, s2, _ = lagged(m, u, 2)
                if live(m, k):
                    act.wait_ge(s_e, k + 1)
                    if late(m, k):
                        act.wait_ge(s_et, k)
                    act.activation(eb.rearrange("p (s c) -> p s c", c=D),
                                   es[:, s2 * SPC:(s2 + 1) * SPC].unsqueeze(2).to_broadcast([P, SPC, D]),
                                   ACT.Copy).then_inc(s_eb, 1)

            act.wait_ge(s_tab, 4)
            run_steps(act, 3, step0)

            def join_exp(L):
                act.wait_ge(L["join_ready"], 1)
                act.activation(join[:, 6:8], join[:, 4:6], ACT.Exp).then_inc(L["join_exp"], 1)

            def std(L, g):
                act.wait_ge(L["var_ready"], g + 1)
                act.activation(mean[:, 2 * GT:3 * GT], mean[:, GT:2 * GT], ACT.Sqrt).then_inc(L["std_ready"], 1)

            L = layers[0]
            join_exp(L)
            with act.Fori(0, NG) as g:
                act.wait_ge(L["prodT"], g + 1)
                act.activation(prodT[0:D, :], ps[0:D, 1 * 512:1 * 512 + GT * P], ACT.Copy).then_inc(L["prodTs"], 1)
                std(L, g)
                act.wait_ge(L["x1T"], g + 1)
                act.activation(prodT[0:D, :], ps[0:D, 1 * 512:1 * 512 + GT * P], ACT.Copy).then_inc(L["x1Ts"], 1)
                act.wait_ge(L["h_product"], g + 1)
                act.activation(hs[:, ds(g * GT, GT), :], bank(4, 0, GT * D).rearrange("p (t c) -> p t c", c=D), ACT.Copy).then_inc(L["h_ready"], 1)
                act.activation(hT[:, :], ps[0:D, 5 * 512:5 * 512 + GT * P], ACT.Copy).then_inc(L["hT_ready"], 1)
                act.wait_ge(L["hl_product"], g + 1)
                act.activation(hl[:, ds(g * GT, GT), :], bank(7, 0, GT * D).rearrange("p (t c) -> p t c", c=D), ACT.Copy).then_inc(L["layer_done"], 1)

            def step1(m, u):
                L = layers[1]
                copy_params(L, m, u)
                k, _, _, s2, n2 = lagged(m, u, 2)
                if live(m, k):
                    act.wait_ge(s_exT, k + 1)
                    if late(m, n2):
                        act.wait_ge(L["sum_done"], k - 1)
                    act.activation(V[s2][:, :, D:P], bank(4).rearrange("p (s c) -> p s c", c=D), ACT.Copy).then_inc(s_den, 1)
                exp_fac(L, m, u, 2)
                k, _, _, s2, n2 = lagged(m, u, 0)
                if live(m, k):
                    act.wait_ge(s_edT, k + 1)
                    if late(m, n2):
                        act.wait_ge(s_ehe, k - 1)
                    act.activation(edT[s2], bank(0), ACT.Copy).then_inc(s_edTs, 1)
                k, _, _, s2, n2 = lagged(m, u, 1)
                if live(m, k):
                    act.wait_ge(s_xsub, k + 1)
                    if late(m, n2):
                        act.wait_ge(s_exT, k - 1)
                    act.activation(Ex[s2], Xs, ACT.Exp).then_inc(s_ex, 1)

            run_steps(act, 3, step1)
            L = layers[1]
            join_exp(L)
            with act.Fori(0, NG) as g:
                std(L, g)

        @block.tensor
        def _(pe):
            pe.wait_ge(s_const, NCONST)
            pe.wait_ge(s_x, 32)
            for q in range(-(-NPAD // 512)):
                if q >= 4:
                    pe.wait_ge(s_xTs, q - 3)
                for t in range(4 * q, min(4 * q + 4, NT)):
                    last = pe.transpose(bank(4 + q % 4, (t % 4) * P, (t % 4 + 1) * P)[0:D, :], xs[:, t, :], ident[:, :])
                last.then_inc(s_xT, 1)
            pe.wait_ge(s_w, 16 * 12)
            for i, w in enumerate((wW1, wW2, wWfc)):
                pe.transpose(bank(0, i * D, (i + 1) * D)[0:D, :], w, ident[0:D, 0:D])
            pe.transpose(bank(0, 3 * D, 4 * D), wWfcr, ident[0:D, 0:D])
            pe.matmul(bank(0, 4 * D, 4 * D + 2)[0:D + 1, :], wAtt, wa, start=True, stop=True).then_inc(s_wT, 1)
            pe.wait_ge(s_wS, 1)
            for n in range(3):
                pe.wait_ge(s_rowf, n + 1)
                for b in range(BLK):
                    q = min(P, T - b * P)
                    last = pe.transpose(ps[:, b * P:b * P + q], rowf[0:q, b, :], ident[0:q, 0:q])
                last.then_inc(s_rowT, 1)
                if n == 0:
                    pe.wait_ge(s_tab, 1)
                    pe.wait_ge(s_xTs, -(-NPAD // 512))
                    for b in range(-(-T // 512)):
                        w = min(512, T - b * 512)
                        last = pe.matmul(bank(4 + b, 0, w), ones[0:1, :], dT[0:1, b * 512:b * 512 + w], start=True, stop=True)
                    last.then_inc(s_bc, 1)
                    pe.wait_ge(s_tab, 2)
                else:
                    pe.wait_ge(s_tab, n + 2)
            for t in range(NT):
                last = pe.matmul(bank(6, 2 * t, 2 * t + 2), xT[0:D + 1, t * P:(t + 1) * P], vc[:, :], start=True, stop=True)
            last.then_inc(s_sps, 1)
            for q in range(-(-NPAD // 512)):
                w = min(512, NPAD - q * 512)
                if q >= 2:
                    pe.wait_ge(s_sds, q - 1)
                pe.matmul(bank(4 + q % 2, 0, w), vc[:, 1:2].to_broadcast([D + 1, P]), xT[0:D + 1, q * 512:q * 512 + w],
                          start=True, stop=True).then_inc(s_sd, 1)

            def fac_products(L, m, u, lag):
                k, _, _, s2, n2 = lagged(m, u, lag)
                if live(m, k):
                    pe.wait_ge(L["drop_ready"], k + 1)
                    if late(m, k):
                        pe.wait_ge(L["fac_ready"], k)
                    for h in range(2):
                        last = pe.matmul(bank(7, h, h + 1), pick[:, h, :], drop[:, s2:s2 + 1], start=True, stop=True)
                    last.then_inc(L["fac_product"], 1)

            def sums(L, m, u, lag, lhs, slots, rows_):
                k, s4, _, s2, _ = lagged(m, u, lag)
                if live(m, k):
                    pe.wait_ge(L["onehot_ready"], (k + 1) * SPC)
                    if late(m, k):
                        pe.wait_ge(L["acc_done"], k * SPC)
                    b = s4 if slots == 4 else s2
                    apart(pe)
                    reach, = chunk_meta(pe, k, 1)
                    with pe.If(reach < NW):
                        for s in range(SPC):
                            last = pe.matmul(bank(5 + s % 2, 0, NW)[0:rows_, :], lhs[b][:, s, 0:rows_],
                                             oh[s2][:, s, 0:NW], start=s < 2, stop=s >= SPC - 2)
                        last.then_inc(L["sum_done"], 1)
                    with pe.Else():
                        for s in range(SPC):
                            last = pe.matmul(bank(5 + s % 2, s // 2 * P, (s // 2 + 1) * P)[0:rows_, :], lhs[b][:, s, 0:rows_],
                                             oh[s2][:, s, :], start=True, stop=True)
                        last.then_inc(L["sum_done"], 1)

            def step0(m, u):
                L = layers[0]
                k, _, _, s2, _ = lagged(m, u, 2)
                if live(m, k):
                    pe.wait_ge(s_eb, k + 1)
                    if late(m, k):
                        pe.wait_ge(L["fwd_done"], k)
                    for i in range(TPC):
                        last = pe.matmul(bank(0, i * P, (i + 1) * P), eb[:, i * P:(i + 1) * P], ident[:, :], start=True, stop=True)
                    last.then_inc(s_et, 1)
                sums(L, m, u, 3, z0, 4, D + 1)
                k, _, _, s2, _ = lagged(m, u, 2)
                if live(m, k):
                    pe.wait_ge(L["max_done"], k + 1)
                    if late(m, k - 1):
                        pe.wait_ge(s_pd, k - 1)
                    for i in range(TPC):
                        last = pe.matmul(bank(2 + s2, 2 * i, 2 * i + 2), M[s2][:, i * P:(i + 1) * P],
                                         ident[:, 0:P:D], start=True, stop=True)
                    last.then_inc(s_mt, 1)
                fac_products(L, m, u, 2)

            pe.wait_ge(s_tab, 5)
            run_steps(pe, 3, step0)

            def join_products(L):
                pe.wait_ge(L["bnd_done"], NCH)
                pe.wait_ge(L["fac_ready"], NCH)
                pe.matmul(bank(7, 100, 101), pick[:, 0, :], F[(NCH - 1) % 2][:, CH - 1:CH], start=True, stop=True)
                pe.matmul(bank(7, 101, 102), pick[:, 1, :], bndM[:, (NCH - 1) % 2:(NCH - 1) % 2 + 1], start=True, stop=True).then_inc(L["join_product"], 1)

            L = layers[0]
            join_products(L)
            with pe.Fori(0, NG) as g:
                pe.wait_ge(L["merged"], g + 1)
                for t in range(GT):
                    last = pe.matmul(bank(0, t * (D + 1), (t + 1) * (D + 1)), merged[0:D + 1, t * P:(t + 1) * P], W1b[:, :], start=True, stop=True)
                last.then_inc(L["n_product"], 1)
                pe.wait_ge(L["xn_ready"], g + 1)
                apart(pe)
                for t in range(GT):
                    last = pe.transpose(ps[0:D, 512 + t * P:512 + (t + 1) * P], n2[:, t * D:(t + 1) * D], ident[:, :])
                last.then_inc(L["prodT"], 1)
                pe.wait_ge(L["prodTs"], g + 1)
                for t in range(GT):
                    last = pe.matmul(bank(3, t * D, (t + 1) * D), prodT[:, t * P:(t + 1) * P], W2b[:, :], start=True, stop=True)
                last.then_inc(L["w2_product"], 1)
                pe.wait_ge(L["x1_ready"], g + 1)
                apart(pe)
                for t in range(GT):
                    last = pe.transpose(ps[0:D, 512 + t * P:512 + (t + 1) * P], n1[:, t * D:(t + 1) * D], ident[:, :])
                last.then_inc(L["x1T"], 1)
                pe.wait_ge(L["x1Ts"], g + 1)
                for t in range(GT):
                    pe.matmul(bank(4, t * D, (t + 1) * D), prodT[0:D, t * P:(t + 1) * P], WfcT[:, :], start=True, stop=True)
                for c in range(2):
                    w = min(512, GT * P - c * 512)
                    last = pe.matmul(bank(5 + c, 0, w)[0:D, :], WfcT[:, :], prodT[0:D, c * 512:c * 512 + w], start=True, stop=True)
                last.then_inc(L["h_product"], 1)
                pe.wait_ge(L["hT_ready"], g + 1)
                for t in range(GT):
                    last = pe.matmul(bank(7, t * D, (t + 1) * D), hT[:, t * P:(t + 1) * P], loopS[:, :], start=True, stop=True)
                last.then_inc(L["hl_product"], 1)

            def step1(m, u):
                L = layers[1]
                k, _, _, s2, n2 = lagged(m, u, 1)
                if live(m, k):
                    pe.wait_ge(s_edTs, k + 1)
                    if late(m, k):
                        pe.wait_ge(s_xsub, k)
                    pe.matmul(bank(1), BD[:, :], edT[s2], start=True, stop=True).then_inc(s_eh, 1)
                k, _, _, s2, _ = lagged(m, u, 2)
                if live(m, k):
                    pe.wait_ge(s_ex, k + 1)
                    if late(m, k):
                        pe.wait_ge(s_den, k)
                    for i in range(TPC):
                        last = pe.transpose(bank(4, i * P, (i + 1) * P), Ex[s2][:, i * P:(i + 1) * P], ident[:, :])
                    last.then_inc(s_exT, 1)
                fac_products(L, m, u, 2)
                k, _, _, s2, n2 = lagged(m, u, 0)
                if live(m, k):
                    pe.wait_ge(s_ed[s2], n2 * 32 + 16 * edge_loads(m, k))
                    if late(m, k):
                        pe.wait_ge(s_edTs, k)
                    for i in range(TPC):
                        last = pe.transpose(bank(0, i * P, (i + 1) * P), ed[s2][:, i * P:(i + 1) * P], ident[:, :])
                    last.then_inc(s_edT, 1)
                k, _, _, s2, n2 = lagged(m, u, 1)
                if live(m, k):
                    if late(m, n2):
                        pe.wait_ge(s_y, k - 1)
                    for i in range(TPC):
                        last = pe.matmul(bank(2 + s2, i * P, (i + 1) * P), edT[s2][:, i * P:(i + 1) * P], BD[:, :], start=True, stop=True)
                    last.then_inc(s_ehe, 1)
                k, _, _, s2, n2 = lagged(m, u, 3)
                if live(m, k):
                    pe.wait_ge(s_val, k + 1)
                sums(L, m, u, 3, V, 2, P)

            pe.wait_ge(layers[0]["layer_done"], NG + 1)
            run_steps(pe, 3, step1)
            L = layers[1]
            join_products(L)
            with pe.Fori(0, NG) as g:
                pe.wait_ge(L["merged"], g + 1)
                for t in range(GT):
                    last = pe.transpose(ps[:, t * P:(t + 1) * P], merged[:, t * P:(t + 1) * P], ident[:, :])
                last.then_inc(L["n_product"], 1)

        @block.vector
        def _(dve):
            chain = Chain(dve, s_dve)
            dve.wait_ge(s_const, NCONST)
            dve.memset(prodT[D:D + 1, :], 1.0)
            dve.tensor_copy(iota[:, :], iota_i[:, :])
            for h in range(2):
                dve.tensor_copy(pick[:, h, :].rearrange("p (a c) -> p a c", a=2),
                                ident[:, h * D:(h + 1) * D].unsqueeze(1).to_broadcast([P, 2, D]))
            dve.memset(rows[:, BLK - 1, :], N).then_inc(s_pads, 1)
            dve.wait_ge(s_drow, 16 * 5)
            rf = rowf.rearrange("p b j -> p (b j)")[:, 0:T]
            chain(dve.tensor_tensor(rf, drow[:, 1:T + 1], drow[:, 0:T], ALU.not_equal))
            chain(dve.tensor_scalar(negs, rf, -BIG, None, ALU.mult))
            dve.sem_inc(s_negs, 1)
            dve.wait_ge(s_wT, 1)
            dve.tensor_copy(W1b[0:D, 0:D], bank(0, 0, D)[0:D, :])
            dve.memset(W1b[D:D + 1, D:D + 1], 1.0)
            dve.tensor_copy(W2b[0:D, :], bank(0, D, 2 * D)[0:D, :])
            dve.tensor_copy(WfcT[:, :], bank(0, 2 * D, 3 * D)[0:D, :])
            dve.tensor_copy(BD[0:D, 0:D], bank(0, 3 * D, 4 * D)[0:D, :])
            dve.tensor_copy(BD[D:P, D:P], bank(0, 3 * D, 4 * D)[D:P, :])
            chain(dve.tensor_copy(vc[:, :], bank(0, 4 * D, 4 * D + 2)[0:D + 1, :]))
            dve.memset(xT[D:D + 1, 0:NPAD], 1.0).then_inc(s_wS, 1)

            metas = meta[:, :].rearrange("p (k n) -> p k n", n=META)

            def halves(t):
                return [t.rearrange("p (t h) -> p h t", h=2)[:, h, :] for h in range(2)]

            for n in range(3):
                dve.wait_ge(s_rows, 48 * (n + 1))
                chain(dve.tensor_copy(rowf, rows))
                dve.sem_inc(s_rowf, 1)
                if n < 2:
                    dve.memset(rows[:, BLK - 1, :], 1 - n).then_inc(s_pads, 1)
                dve.wait_ge(s_rowT, n + 1)
                if n == 0:
                    chain(dve.tensor_copy(dT, ps[:, 0:T]))
                    dve.sem_inc(s_tab, 1)
                    dve.wait_ge(s_bc, 1)
                    for h in range(2):
                        dve.tensor_tensor(halves(relT)[h], dT[:, h * HT:(h + 1) * HT],
                                          ps[:, 2048 + h * HT:2048 + (h + 1) * HT], ALU.subtract)
                        first = ps[:, 2048 + h * HT:2048 + (h + 1) * HT:TPC]
                        dve.tensor_tensor(halves(relC)[h].rearrange("p (k i) -> p k i", i=TPC),
                                          dT[:, h * HT:(h + 1) * HT].rearrange("p (k i) -> p k i", i=TPC),
                                          first.unsqueeze(2).to_broadcast([P, NCH, TPC]), ALU.subtract)
                        row = dT[0:1, h * HT:(h + 1) * HT].rearrange("p (k i) -> p k i", i=TPC)
                        dve.tensor_copy(metas[:, :, 1:1 + SPC].rearrange("p k (i h) -> p h k i", h=2)[:, h, :, :], row)
                        nxt = dT[0:1, (h + 1) * HT - (NCH - 1) * TPC:(h + 1) * HT:TPC] if h else dT[0:1, TPC:HT + 1:TPC]
                        n_next = NCH - h
                        dve.tensor_tensor(reach2[:, h, 0:n_next], nxt, dT[0:1, h * HT:h * HT + (n_next - 1) * TPC + 1:TPC], ALU.subtract)
                    dve.tensor_scalar(reach2[:, 1, NCH - 1:NCH], dT[0:1, T - TPC:T - TPC + 1], -1.0, float(N), ALU.mult, ALU.add)
                    chain(dve.tensor_copy(join[:, 0:1], ps[:, 2048 + HT:2048 + HT + 1]))
                    chain(dve.tensor_tensor(metas[:, :, 0], reach2[:, 0, :], reach2[:, 1, :], ALU.max))
                    chain(dve.tensor_scalar(bnd[:, :], ps[:, 2048 + HT:2048 + T:TPC], join[:, 0:1], -BIG,
                                            ALU.not_equal, ALU.mult))
                elif n == 1:
                    for h in range(2):
                        last = dve.tensor_scalar(halves(biasT)[h], ps[:, h * HT:(h + 1) * HT], 0.0, 0.625, ALU.is_equal, ALU.mult)
                    chain(last)
                else:
                    for h in range(2):
                        last = dve.tensor_copy(halves(srcT)[h], ps[:, h * HT:(h + 1) * HT])
                    chain(last)
                dve.sem_inc(s_tab, 1)
            dve.wait_ge(s_x, 32)
            dve.tensor_copy(xtb[:, :, 0:D], xs[:, :, :])
            dve.memset(xtb[:, :, D:D + 1], 1.0)
            dve.wait_ge(s_sps, 1)
            chain(dve.tensor_scalar(xtb[:, :, D + 1:D + 2], bank(6, 0, 2 * NT).rearrange("p (t c) -> p t c", c=2)[:, :, 0:1],
                                    0.125, None, ALU.mult))
            dve.sem_inc(s_xtb, 1)
            dve.wait_ge(s_sds, -(-NPAD // 512))
            dve.memset(sdst[:, NPAD:ACCW], 0.0)
            chain(dve.memset(acc[0][:, :], 0.0))
            dve.sem_inc(s_tab, 1)
            dve.wait_ge(s_cont, 16)

            def scans(L, m, u, lag, scores):
                k, _, _, s2, n2 = lagged(m, u, lag)
                dve.wait_ge(L[f"neg_loaded_{s2}"], (n2 + 1) * 32)
                first = -BIG if isinstance(k, int) and k == 0 else F[1 - s2][:, CH - 1:CH]
                if late(m, k - 1):
                    dve.wait_ge(L["bnd_done"], k)
                dve.tensor_tensor_scan(F[s2], neg[s2][:, 0:CH], scores, first, ALU.add, ALU.max).then_inc(L["fwd_done"], 1)
                dve.wait_ge(L["fwd_done"], k + 1)
                dve.tensor_tensor_scan(M[s2][:, ::-1], neg[s2][:, CH:0:-1], F[s2][:, ::-1], F[s2][:, CH - 1:CH],
                                       ALU.add, ALU.max).then_inc(L["max_done"], 1)
                dve.wait_ge(L["max_done"], k + 1)
                prev = -BIG if isinstance(k, int) and k == 0 else F[1 - s2][:, CH - 1:CH]
                if late(m, n2):
                    dve.wait_ge(L["fac_product"], k - 1)
                if isinstance(k, int) and k == 0:
                    dve.memset(drop[:, 0:1], 0.0).then_inc(L["drop_ready"], 1)
                else:
                    dve.tensor_scalar(drop[:, s2:s2 + 1], M[s2][:, 0:1], prev, 0.0, ALU.subtract, ALU.max).then_inc(L["drop_ready"], 1)
                dve.scalar_tensor_tensor(bndM[:, s2:s2 + 1], M[s2][:, 0:1], bnd[:, ds(k, 1)], bndM[:, 1 - s2:2 - s2],
                                         ALU.add, ALU.max).then_inc(L["bnd_done"], 1)

            def add_windows(L, m, u, lag, rows_):
                k, _, _, s2, _ = lagged(m, u, lag)
                if not live(m, k):
                    return
                dve.wait_ge(L["sum_done"], k + 1)
                dve.wait_ge(L["fac_ready"], k + 1)
                apart(dve)
                reach, *at_ = chunk_meta(dve, k, 1 + SPC)
                with dve.If(reach < NW):
                    if late(m, k):
                        dve.wait_ge(L["acc_done"], k * SPC)
                    for h in range(2):
                        win = acc[h][0:rows_, ds(at_[h], NW)]
                        dve.scalar_tensor_tensor(win, win, fac[0:rows_, 2 * s2 + h:2 * s2 + h + 1], bank(5 + h, 0, NW)[0:rows_, :],
                                                 ALU.mult, ALU.add).then_inc(L["acc_done"], TPC)
                with dve.Else():
                    for s in range(SPC):
                        h = s % 2
                        win = acc[h][0:rows_, ds(at_[s], P)]
                        new = bank(5 + h, s // 2 * P, (s // 2 + 1) * P)[0:rows_, :]
                        if not (isinstance(k, int) and k == 0 and s < 2):
                            dve.wait_ge(L["acc_done"], k * SPC + s - 1)
                        if s < 2:
                            dve.scalar_tensor_tensor(win, win, fac[0:rows_, 2 * s2 + h:2 * s2 + h + 1], new,
                                                     ALU.mult, ALU.add).then_inc(L["acc_done"], 1)
                        else:
                            dve.tensor_tensor(win, win, new, ALU.add).then_inc(L["acc_done"], 1)

            def step0(m, u):
                L = layers[0]
                k, _, _, s2, n2 = lagged(m, u, 3)
                sl = slice(s2 * SPC, (s2 + 1) * SPC)
                if live(m, k):
                    dve.wait_ge(s_mt, k + 1)
                    if late(m, n2):
                        dve.wait_ge(s_p, k - 1)
                    dve.tensor_tensor(pd[:, sl], es[:, sl], bank(2 + s2, 0, SPC), ALU.subtract).then_inc(s_pd, 1)
                k, s4, n4, s2, n2 = lagged(m, u, 2)
                sl = slice(s2 * SPC, (s2 + 1) * SPC)
                if live(m, k):
                    dve.wait_ge(L[f"z_loaded_{s4}"], (n4 + 1) * (16 * SPC))
                    dve.wait_ge(s_u, (k + 1) * SPC)
                    dve.tensor_tensor(ts[:, sl], us[:, sl], z0[s4][:, :, D + 1], ALU.add).then_inc(s_t, 1)
                    dve.wait_ge(s_t, 2 * k + 1)
                    dve.tensor_tensor(ubb[:, sl], ts[:, sl], table(biasT, k), ALU.add).then_inc(s_t, 1)
                    dve.wait_ge(s_t, 2 * k + 2)
                    if late(m, n2):
                        dve.wait_ge(s_pd, k - 1)
                    dve.scalar_tensor_tensor(es[:, sl], ubb[:, sl], 0.2, ubb[:, sl], ALU.mult, ALU.max).then_inc(s_e, 1)
                k, s4, _, s2, n2 = lagged(m, u, 3)
                if live(m, k):
                    dve.wait_ge(s_p, k + 1)
                    if late(m, n2):
                        dve.wait_ge(L["sum_done"], k - 1)
                    apart(dve)
                    reach, = chunk_meta(dve, k, 1)
                    with dve.If(reach < NW):
                        dve.tensor_tensor(oh[s2][:, :, 0:NW], ohn[s4], pe_[:, s2 * SPC:(s2 + 1) * SPC].unsqueeze(2).to_broadcast([P, SPC, NW]),
                                          ALU.mult).then_inc(L["onehot_ready"], SPC)
                    with dve.Else():
                        for s in range(SPC):
                            dve.tensor_scalar(oh[s2][:, s, :], iota[:, :], relb[s4][:, s:s + 1],
                                              pe_[:, s2 * SPC + s:s2 * SPC + s + 1], ALU.is_equal, ALU.mult).then_inc(L["onehot_ready"], 1)
                k, s4, _, s2, _ = lagged(m, u, 1)
                if live(m, k):
                    dve.wait_ge(L["rel_ready"], 2 * k + 2)
                    apart(dve)
                    reach, *at_ = chunk_meta(dve, k, 1 + SPC)
                    mine = us[:, s2 * SPC:(s2 + 1) * SPC]
                    with dve.If(reach < NW):
                        dve.tensor_tensor(ohn[s4], iota[:, 0:NW].unsqueeze(1).to_broadcast([P, SPC, NW]),
                                          relc[s4][:, :].unsqueeze(2).to_broadcast([P, SPC, NW]), ALU.is_equal).then_inc(s_u, 1)
                        dve.wait_ge(s_u, k * SPC + 1)
                        both = junk.rearrange("p (i h w) -> p h i w", h=2, w=NW)
                        for h in range(2):
                            dve.tensor_tensor(both[:, h, :, :], ohn[s4].rearrange("p (i h) w -> p h i w", h=2)[:, h, :, :],
                                              sdst[:, ds(at_[h], NW)].unsqueeze(1).to_broadcast([P, TPC, NW]), ALU.mult).then_inc(s_u, 1)
                        dve.wait_ge(s_u, k * SPC + 3)
                        dve.tensor_reduce(mine, junk.rearrange("p (s w) -> p s w", w=NW), AX.X, ALU.add).then_inc(s_u, SPC - 3)
                    with dve.Else():
                        for s in range(SPC):
                            if not (isinstance(k, int) and k == 0 and s < 2):
                                dve.wait_ge(s_u, k * SPC + s - 1)
                            dve.scalar_tensor_tensor(junk[:, s % 2 * P:(s % 2 + 1) * P], iota[:, :], relb[s4][:, s:s + 1],
                                                     sdst[:, ds(at_[s], P)], ALU.is_equal, ALU.mult,
                                                     accum_out=mine[:, s:s + 1]).then_inc(s_u, 1)
                k, _, _, s2, _ = lagged(m, u, 2)
                if live(m, k):
                    dve.wait_ge(s_et, k + 1)
                    if late(m, k - 1):
                        dve.wait_ge(s_mt, k - 1)
                    scans(L, m, u, 2, bank(0))
                add_windows(L, m, u, 3, D + 1)

            run_steps(dve, 3, step0)

            def join_halves(L, rows_, chain):
                dve.wait_ge(L["join_product"], 1)
                dve.wait_ge(L["acc_done"], NCH * SPC)
                chain(dve.tensor_copy(join[:, 0:2], bank(7, 100, 102)))
                chain(dve.tensor_tensor(join[:, 2:3], join[:, 0:1], cont[:, 0:1], ALU.add))
                chain(dve.tensor_tensor(join[:, 3:4], join[:, 2:3], join[:, 1:2], ALU.max))
                chain(dve.tensor_tensor(join[:, 4:5], join[:, 2:3], join[:, 3:4], ALU.subtract))
                chain(dve.tensor_tensor(join[:, 5:6], join[:, 1:2], join[:, 3:4], ALU.subtract))
                dve.sem_inc(L["join_ready"], 1)
                dve.wait_ge(L["join_exp"], 1)
                apart(dve)
                at_ = chunk_meta(dve, 0, 3)[2:]
                for h in range(2):
                    one = acc[h][0:rows_, ds(at_[0], 1)]
                    chain(dve.tensor_scalar(one, one, join[0:rows_, 6 + h:7 + h], None, ALU.mult))

            def layernorm(L, chain, g, y, t1, t2, res):
                yv, tv, rv = (t.rearrange("p (t c) -> p t c", c=D) for t in (y, t1, res))
                chain(dve.tensor_reduce(mean[:, 0:GT], yv, AX.X, ALU.add))
                chain(dve.tensor_scalar(mean[:, 0:GT], mean[:, 0:GT], 1.0 / D, None, ALU.mult))
                chain(dve.tensor_tensor(tv, yv, mean[:, 0:GT].unsqueeze(2).to_broadcast([P, GT, D]), ALU.subtract))
                chain(dve.tensor_tensor(t2, t1, t1, ALU.mult))
                chain(dve.tensor_reduce(mean[:, 3 * GT:4 * GT], t2.rearrange("p (t c) -> p t c", c=D), AX.X, ALU.add))
                dve.tensor_scalar(mean[:, GT:2 * GT], mean[:, 3 * GT:4 * GT], 1.0 / D, 1e-5, ALU.mult, ALU.add).then_inc(L["var_ready"], 1)
                dve.wait_ge(L["std_ready"], g + 1)
                chain(dve.reciprocal(mean[:, 0:GT], mean[:, 2 * GT:3 * GT]))
                return tv, mean[:, 0:GT].unsqueeze(2).to_broadcast([P, GT, D])

            L = layers[0]
            chain = Chain(dve, L["dve_epi"])
            join_halves(L, D + 1, chain)
            c0 = chain.n
            PER0 = 17
            with dve.Fori(0, NG) as g:
                chain = Chain(dve, L["dve_epi"], g * PER0 + c0)
                xg = xs[:, ds(g * GT, GT), :]
                v3 = lambda t: t.rearrange("p (t c) -> p t c", c=D)
                dve.tensor_tensor(merged[0:D + 1, :], acc[0][0:D + 1, ds(g * (GT * P), GT * P)],
                                  acc[1][0:D + 1, ds(g * (GT * P), GT * P)], ALU.add).then_inc(L["merged"], 1)
                dve.wait_ge(L["n_product"], g + 1)
                nb = bank(0, 0, GT * (D + 1)).rearrange("p (t c) -> p t c", c=D + 1)
                chain(dve.tensor_scalar(mean[:, 0:GT], nb[:, :, D], 1e-9, None, ALU.add))
                chain(dve.reciprocal(mean[:, 0:GT], mean[:, 0:GT]))
                chain(dve.tensor_tensor(v3(n1), nb[:, :, 0:D], mean[:, 0:GT].unsqueeze(2).to_broadcast([P, GT, D]), ALU.mult))
                dve.tensor_tensor(v3(n2), v3(n1), xg, ALU.mult).then_inc(L["xn_ready"], 1)
                chain(dve.tensor_tensor(v3(n3), v3(n1), xg, ALU.add))
                dve.wait_ge(L["w2_product"], g + 1)
                chain(dve.tensor_tensor(n4, n3, bank(3, 0, GT * D), ALU.add))
                chain(dve.scalar_tensor_tensor(n3, n4, 0.2, n4, ALU.mult, ALU.max))
                chain(dve.tensor_tensor(v3(n4), v3(n3), xg, ALU.add))
                tv, r = layernorm(L, chain, g, n4, n3, n2, n1)
                chain(dve.tensor_tensor(v3(n1), tv, r, ALU.mult))
                apart(dve)
                chain(dve.tensor_copy(xg, v3(n1)))
                dve.sem_inc(L["x1_ready"], 1)
                dve.wait_ge(L["x1T"], g + 1)
                chain(dve.memset(rden[:, 0:1], 0.0))
                while chain.n < PER0:
                    chain(dve.memset(rden[:, 0:1], 0.0))
                assert chain.n == PER0, chain.n
            chain = Chain(dve, L["dve_epi"], NG * PER0 + c0)
            chain(dve.memset(acc[0][:, :], 0.0))
            chain(dve.memset(acc[1][:, :], 0.0))
            chain(dve.memset(bndM[:, :], -BIG))
            dve.sem_inc(L["layer_done"], 1)

            def step1(m, u):
                L = layers[1]
                k, _, _, s2, _ = lagged(m, u, 1)
                if live(m, k):
                    dve.wait_ge(s_eh, k + 1)
                    scans(L, m, u, 1, bank(1))
                    if late(m, k):
                        dve.wait_ge(s_ex, k)
                    dve.tensor_tensor(Xs, bank(1), M[s2], ALU.subtract).then_inc(s_xsub, 1)
                k, s4, n4, s2, n2 = lagged(m, u, 2)
                if live(m, k):
                    dve.wait_ge(L[f"z_loaded_{s4}"], (n4 + 1) * (16 * SPC))
                    dve.wait_ge(s_ehe, k + 1)
                    if late(m, k):
                        dve.wait_ge(s_val, k)
                    dve.tensor_tensor(Y, bank(2 + s2), z[s4][:, 0:SPC * D], ALU.add).then_inc(s_y, 1)
                    dve.wait_ge(L["rel_ready"], 2 * k + 2)
                    if late(m, n2):
                        dve.wait_ge(L["sum_done"], k - 1)
                    apart(dve)
                    reach, = chunk_meta(dve, k, 1)
                    with dve.If(reach < NW):
                        dve.tensor_tensor(oh[s2][:, :, 0:NW], iota[:, 0:NW].unsqueeze(1).to_broadcast([P, SPC, NW]),
                                          relc[s4][:, :].unsqueeze(2).to_broadcast([P, SPC, NW]), ALU.is_equal
                                          ).then_inc(L["onehot_ready"], SPC)
                    with dve.Else():
                        for s in range(SPC):
                            dve.tensor_scalar(oh[s2][:, s, :], iota[:, :], relb[s4][:, s:s + 1], None,
                                              ALU.is_equal).then_inc(L["onehot_ready"], 1)
                    dve.wait_ge(s_den, k + 1)
                    dve.wait_ge(s_y, k + 1)
                    dve.tensor_tensor(V[s2][:, :, 0:D], V[s2][:, :, D:P], Y.rearrange("p (s c) -> p s c", c=D),
                                      ALU.mult).then_inc(s_val, 1)
                add_windows(L, m, u, 3, P)

            run_steps(dve, 3, step1)

            L = layers[1]
            chain = Chain(dve, L["dve_epi"])
            join_halves(L, P, chain)
            c1 = chain.n
            PER1 = 16
            with dve.Fori(0, NG) as g:
                chain = Chain(dve, L["dve_epi"], g * PER1 + c1)
                hg, hlg, xg = (t[:, ds(g * GT, GT), :] for t in (hs, hl, xs))
                dve.tensor_tensor(merged, acc[0][:, ds(g * (GT * P), GT * P)],
                                  acc[1][:, ds(g * (GT * P), GT * P)], ALU.add).then_inc(L["merged"], 1)
                dve.wait_ge(L["n_product"], g + 1)
                nb = ps[:, 0:GT * P].rearrange("p (t c) -> p t c", c=P)
                chain(dve.tensor_copy(v3(n3), nb[:, :, D:P]))
                chain(dve.tensor_scalar(n4, n3, 1e-30, None, ALU.max))
                chain(dve.reciprocal(n4, n4))
                chain(dve.tensor_tensor(v3(n1), nb[:, :, 0:D], v3(n4), ALU.mult))
                chain(dve.tensor_tensor(v3(n2), v3(n1), hlg, ALU.add))
                apart(dve)
                chain(dve.tensor_copy(n1, hg.rearrange("p t c -> p (t c)")))
                apart(dve)
                chain(dve.copy_predicated(n1, n3.bitcast(u32), n2))
                chain(dve.scalar_tensor_tensor(v3(n4), v3(n1), 0.0, xg, ALU.max, ALU.add))
                tv, r = layernorm(L, chain, g, n4, n3, n2, n1)
                chain(dve.tensor_tensor(hg, tv, r, ALU.mult))
                while chain.n < PER1:
                    chain(dve.memset(rden[:, 0:1], 0.0))
                assert chain.n == PER1, chain.n
            dve.sem_inc(L["layer_done"], 1)


_INS = ['x', 'src', 'dst', 'edge_attr_64', 'edge_type_4', 'L0_gnn_W1_w', 'L0_gnn_W1_b', 'L0_gnn_W2_w', 'L0_gnn_W2_b',
        'L0_gnn_W_att_w', 'L0_gnn_W_att_b', 'L0_gnn_a', 'L1_gnn_W_fc', 'L1_gnn_W_fcr', 'L1_gnn_loop_W']
_OUTS = [((N, D), 'float32')]


def kernel(**inputs):
    import numpy as _np
    import concourse.bacc as _bacc
    from concourse import mybir as _mybir
    from concourse.bass_utils import run_bass_kernel_spmd as _run

    nc = _bacc.Bacc("TRN2", target_bir_lowering=False, num_devices=1)
    arrays, args = {}, []
    for name in _INS:
        a = _np.ascontiguousarray(inputs[name])
        arrays[f"in_{name}_dram"] = a
        args.append(nc.dram_tensor(f"in_{name}_dram", a.shape, _mybir.dt.from_np(a.dtype), kind="ExternalInput").ap())
    for i, (shape, dtype) in enumerate(_OUTS):
        dt = _mybir.dt.from_np(_np.dtype(dtype))
        args.append(nc.dram_tensor(f"out_{i}_dram", shape, dt, kind="ExternalOutput").ap())
    gnn_kernel(nc, *args)
    r = _run(nc, [arrays], core_ids=[0])
    got = tuple(r.results[0][f"out_{i}_dram"] for i in range(len(_OUTS)))
    return got[0]
```

```python
import concourse.bass as bass
from concourse import mybir
from contextlib import ExitStack

P = 128
D = 64
N = 6250
E = 206250
TPC = 4
CH = TPC * P
NCH = -(-E // (2 * CH))
HT = NCH * TPC
HALF = HT * P
T = 2 * HT
SPC = 2 * TPC
NT = -(-N // P)
NPAD = NT * P
ACCW = NPAD + P
GT = 7
NG = NT // GT
XW = D + 2
BIG = float(2.0 ** 100)
NW = 32
META = 12
UNROLL = 4
HEAD = 2 * UNROLL
BLK = -(-T // P)


def lagged(m, u, lag):
    d = u - lag
    return m * UNROLL + d, d % 4, m + d // 4, d % 2, m * 2 + d // 2


def live(m, k):
    return not isinstance(m, int) or 0 <= k < NCH


def late(m, count):
    return not isinstance(m, int) or count > 0


def run_steps(eng, lags, step):
    total = NCH + lags
    loops = (NCH - HEAD) // UNROLL
    for s in range(HEAD):
        step(s // UNROLL, s % UNROLL)
    with eng.Fori(HEAD // UNROLL, HEAD // UNROLL + loops) as m:
        for u in range(UNROLL):
            step(m, u)
    for s in range(HEAD + loops * UNROLL, total):
        step(s // UNROLL, s % UNROLL)


def edge_loads(m, k):
    if not isinstance(m, int):
        return 2
    left = min(max(E - HALF - k * CH, 0), CH)
    return 1 + (left >= P) + (left % P > 0)


assert HEAD + (NCH - HEAD) // UNROLL * UNROLL <= (E - HALF) // CH


class Chain:

    def __init__(self, eng, sem, base=0):
        self.eng, self.sem, self.base, self.n = eng, sem, base, 0

    def __call__(self, ins):
        ins.then_inc(self.sem, 1)
        self.n += 1
        self.eng.wait_ge(self.sem, self.base + self.n)


def gnn_kernel(nc, x, src, dst, edge_attr, edge_type, W1, b1, W2, b2, Watt, batt, a, Wfc, Wfcr, loopW, out):
    f32, i32, u32, bf16 = mybir.dt.float32, mybir.dt.int32, mybir.dt.uint32, mybir.dt.bfloat16
    ALU, ACT, AX = mybir.AluOpType, mybir.ActivationFunctionType, mybir.AxisListType
    ds = bass.ds

    xtab = nc.dram_tensor("xtab", (NPAD, XW), f32).ap()
    htab = nc.dram_tensor("htab", (NPAD, D), f32).ap()
    negd = nc.dram_tensor("negd", (2 * HALF,), bf16).ap()

    ctx = ExitStack()
    with ctx:
        def sb(name, shape, dt=f32):
            return ctx.enter_context(nc.sbuf_tensor(name, shape, dt))

        def sem(name):
            return ctx.enter_context(nc.semaphore(name))

        srcT = sb("srcT", [P, T], u32)
        relT = sb("relT", [P, T])
        biasT = sb("biasT", [P, T])
        relC = sb("relC", [P, T])
        meta = sb("meta", [1, NCH * META], i32)
        bnd = sb("bnd", [P, NCH])
        acc = [sb("accA", [P, ACCW]), sb("accB", [P, ACCW])]
        xs = sb("xs", [P, NT, D])
        hh = sb("hh", [P, 2, NT * D])
        hs = hh[:, 0, :].rearrange("p (t c) -> p t c", c=D)
        hl = hh[:, 1, :].rearrange("p (t c) -> p t c", c=D)
        xtb = hh[:, :, :].rearrange("p a b -> p (a b)")[:, 0:NT * XW].rearrange("p (t c) -> p t c", c=XW)
        xT = acc[0]
        ident = sb("ident", [P, P])
        pick = sb("pick", [P, 2, P])
        iota = sb("iota", [P, P])
        iota_i = sb("iota_i", [P, P], i32)
        ones = sb("ones", [1, P])
        W1b = sb("W1b", [D + 1, D + 1])
        W2b = sb("W2b", [D + 1, D])
        WH = sb("WH", [D, P])
        loopS = sb("loopS", [D, D])
        BD = sb("BD", [P, P])
        vc = sb("vc", [D + 1, 2])
        wl = sb("wl", [D, 5 * D + D + 1 + 2])
        wW1, wW2, wWfc = (wl[:, i * D:(i + 1) * D] for i in range(3))
        wWfcr = wl[:, 3 * D:5 * D]
        wAtt = wl[:, 5 * D:6 * D + 1]
        wa = wl[:, 6 * D + 1:6 * D + 3]
        bndM = sb("bndM", [P, 2])
        cont = sb("cont", [P, 1], bf16)
        join = sb("join", [P, 8])

        NF = 10752
        arena = sb("arena", [P, NF])
        at = [0]

        def carve(n, dt=f32):
            w = n if dt in (f32, i32, u32) else -(-n // 2)
            ap = arena[:, at[0]:at[0] + w]
            at[0] += w
            assert at[0] <= NF
            return ap if dt == f32 else ap.bitcast(dt)

        ixb = [sb(f"ixb{i}", [P, SPC], u32) for i in range(4)]
        relb = [sb(f"relb{i}", [P, SPC]) for i in range(4)]
        relc = [sb(f"relc{i}", [P, SPC]) for i in range(4)]
        z = [carve(SPC * XW) for _ in range(4)]
        z0 = [t.rearrange("p (s c) -> p s c", c=XW) for t in z]
        z1 = [t[:, 0:SPC * D].rearrange("p (s c) -> p s c", c=D) for t in z]
        neg = [sb(f"neg{i}", [P, CH + 1], bf16) for i in range(2)]
        F = [carve(CH) for _ in range(2)]
        M = [carve(CH) for _ in range(2)]
        oh = [carve(SPC * P).rearrange("p (s w) -> p s w", w=P) for _ in range(2)]
        drop = sb("drop", [P, 2])
        fac = sb("fac", [P, 4])
        ub = sb("ub", [P, 2 * SPC])
        us = sb("us", [P, 2 * SPC])
        ubb = sb("ubb", [P, 2 * SPC])
        ts = sb("ts", [P, 2 * SPC])
        es = sb("es", [P, 2 * SPC])
        pd = sb("pd", [P, 2 * SPC])
        pe_ = sb("pe_", [P, 2 * SPC])
        junk = carve(SPC * NW)
        ohn = [carve(SPC * NW).rearrange("p (s w) -> p s w", w=NW) for _ in range(4)]
        eb = carve(CH)
        at[0] = 4 * SPC * XW
        share, prod, summed, ybuf, square, x1b = ([carve(GT * D) for _ in range(2)] for _ in range(6))
        no_edge = sb("no_edge", [P, NT])
        merged = [carve(GT * P) for _ in range(2)]
        small = [sb(f"small{i}", [P, 5 * GT]) for i in range(2)]
        prodT = sb("prodT", [D + 1, GT * P])
        x1T = sb("x1T", [D, GT * P])
        big = sb("big", [P, ACCW])
        sdst = big
        at1 = [0]

        def carve1(n):
            ap = big[:, at1[0]:at1[0] + n]
            at1[0] += n
            assert at1[0] <= ACCW
            return ap

        ed = [carve1(CH) for _ in range(2)]
        edT = [carve1(CH) for _ in range(2)]
        Xs = carve1(CH)
        Ex = [carve1(CH) for _ in range(2)]
        Y = carve1(CH)
        V = [carve1(SPC * P).rearrange("p (s c) -> p s c", c=P) for _ in range(2)]
        assert at1[0] <= ACCW
        at[0] = 0
        reach2 = carve(2 * NCH)[0:1, :].rearrange("p (h k) -> p h k", h=2)
        drow = carve(HT * 2 + 1, i32)
        negs = carve(HT * 2, bf16)
        rows = carve(BLK * P, i32).rearrange("p (b j) -> p b j", j=P)
        rowf = carve(BLK * P).rearrange("p (b j) -> p b j", j=P)
        dT = carve(T)

        ps = ctx.enter_context(nc.psum_tensor("ps", [P, 8 * 512], f32))

        def bank(i, a=0, b=512):
            return ps[:, i * 512 + a:i * 512 + b]

        s_const = sem("const_ready")
        s_w = sem("weights_loaded")
        s_x = sem("x_loaded")
        s_drow = sem("dst_flat_loaded")
        s_pads = sem("pads_set")
        s_rows = sem("rows_loaded")
        s_rowf = sem("rows_converted")
        s_rowT = sem("rows_transposed")
        s_tab = sem("table_written")
        s_negs = sem("flags_ready")
        s_negd = sem("flags_stored")
        s_cont = sem("cont_loaded")
        s_bc = sem("bases_broadcast")
        s_wT = sem("weights_transposed")
        s_wS = sem("weights_ready")
        s_xT = sem("x_transposed")
        s_xTs = sem("xT_ready")
        s_sps = sem("node_scores")
        s_sd = sem("sdst_product")
        s_sds = sem("sdst_ready")
        s_xtb = sem("xtab_built")
        s_xtd = sem("xtab_stored")
        s_dve = sem("dve_chain")
        s_act = sem("act_chain")
        layers = []
        for L in range(2):
            layers.append({n: sem(f"{n}{L}") for n in (
                "neg_loaded_0", "neg_loaded_1", "ix_ready", "rel_ready",
                "z_loaded_0", "z_loaded_1", "z_loaded_2", "z_loaded_3",
                "fwd_done", "max_done", "drop_ready", "bnd_done", "fac_product", "fac_ready",
                "onehot_ready", "sum_done", "acc_done", "zero_done",
                "merged", "n_product", "xn_ready", "sum_ready", "prodT", "prodTs", "w2_product", "x1_ready", "x1_kept",
                "x1T", "x1Ts", "h_product", "h_ready", "hl_ready", "h_stored", "rows_done",
                "dve_epi", "centred", "squared", "var_ready", "std_ready", "join_product", "join_done", "join_ready", "join_exp", "layer_done")})
        s_u = sem("u_ready")
        s_e = sem("e_ready")
        s_eb = sem("e_spread")
        s_et = sem("eT_ready")
        s_mt = sem("maxT_ready")
        s_pd = sem("pd_ready")
        s_p = sem("p_ready")
        s_t = sem("t_done")
        s_ed = [sem("edge_loaded_0"), sem("edge_loaded_1")]
        s_edT = sem("edgeT_product")
        s_edTs = sem("edgeT_ready")
        s_eh = sem("ehT_ready")
        s_ehe = sem("eh_ready")
        s_xsub = sem("x_sub")
        s_ex = sem("ex_ready")
        s_exT = sem("exT_product")
        s_den = sem("den_ready")
        s_y = sem("y_ready")
        s_val = sem("values_ready")
        s_out = sem("out_stored")

        NCONST = 14

        s_apart = sem("apart")

        def apart(eng):
            eng.sem_inc(s_apart, 1)

        block = ctx.enter_context(nc.Block())

        def v3(t):
            return t.rearrange("p (t c) -> p t c", c=D)

        def chunk_meta(eng, k, count):
            _, got = nc.values_load_multi_w_load_instructions(
                meta[0:1, ds(k * META, count)], engines=[eng.engine], min_val=0, max_val=N,
                skip_runtime_bounds_check_because="dst values, N for padding, or a difference of two")
            return got

        def table(t, k, step=1):
            return t[:, ds(k * SPC, SPC)]

        @block.sync
        def _(sp):
            for view, w in ((wW1, W1), (wW2, W2), (wWfc, Wfc), (wWfcr[:, 0:D], Wfcr), (wWfcr[:, D:2 * D], Wfcr),
                            (wAtt[:, 0:D], Watt)):
                sp.dma_start(view, w).then_inc(s_w, 16)
            sp.dma_start(wAtt[:, D:D + 1], batt.rearrange("(o i) -> o i", i=1)).then_inc(s_w, 16)
            sp.dma_start(wa[:, 0:1], a[0:D, :]).then_inc(s_w, 16)
            sp.dma_start(wa[:, 1:2], a[D:2 * D, :]).then_inc(s_w, 16)
            sp.dma_start(loopS[:, :], loopW).then_inc(s_w, 16)
            sp.wait_ge(s_const, 1)
            full = (NT - 1) * P
            sp.dma_start(xs[:, 0:NT - 1, :], x[0:full, :].rearrange("(t p) c -> p t c", p=P)).then_inc(s_x, 16)
            sp.dma_start(xs[0:N - full, NT - 1, :], x[full:N, :]).then_inc(s_x, 16)
            sp.wait_ge(s_const, 3)
            sp.dma_start(W1b[D:D + 1, 0:D], b1.rearrange("(i o) -> i o", i=1)).then_inc(s_w, 16)
            sp.dma_start(W2b[D:D + 1, :], b2.rearrange("(i o) -> i o", i=1)).then_inc(s_w, 16)
            sp.wait_ge(s_const, 5)
            EP = T
            full = E // EP
            for lo, hi in ((0, full // 16 * 16), (full // 16 * 16, full)):
                sp.dma_start(drow[lo:hi, 1:EP + 1],
                             dst[lo * EP:hi * EP].rearrange("(p e) -> p e", e=EP)).then_inc(s_drow, 16)
            sp.dma_start(drow[full:full + 1, 1:E - full * EP + 1],
                         dst[full * EP:E].rearrange("(p e) -> p e", p=1)).then_inc(s_drow, 16)
            last = dst[0:(P - 1) * EP].rearrange("(p e) -> p e", e=EP)[:, EP - 1:EP]
            with nc.allow_non_contiguous_dma(reason="one element per partition"):
                sp.dma_start(drow[1:113, 0:1], last[0:112, :]).then_inc(s_drow, 16)
                sp.dma_start(drow[113:P, 0:1], last[112:P - 1, :]).then_inc(s_drow, 16)
            for n, arr in enumerate((dst, edge_type, src)):
                sp.wait_ge(s_pads, n + 1)
                whole = E // P // P * P
                nb = whole // P
                sp.dma_start(rows[:, 0:nb, :], arr[0:whole * P].rearrange("(b q j) -> q b j", q=P, j=P)).then_inc(s_rows, 16)
                rest = E // P - whole
                sp.dma_start(rows[0:rest, nb, :],
                             arr[whole * P:(whole + rest) * P].rearrange("(q j) -> q j", j=P)).then_inc(s_rows, 16)
                sp.dma_start(rows[rest:rest + 1, nb, 0:E % P],
                             arr[(whole + rest) * P:E].rearrange("(q j) -> q j", q=1)).then_inc(s_rows, 16)
            sp.wait_ge(s_negs, 1)
            sp.dma_start(negd.rearrange("(p e) -> p e", p=P), negs).then_inc(s_negd, 16)
            sp.wait_ge(s_xtb, 1)
            sp.dma_start(xtab.rearrange("(t p) c -> p t c", p=P), xtb).then_inc(s_xtd, 16)
            sp.wait_ge(s_negd, 16)
            sp.dma_start(cont[:, :], negd[HALF:HALF + 1].rearrange("(a b) -> a b", b=1).to_broadcast([P, 1])).then_inc(s_cont, 16)

            def load_flags(L, m, u):
                k, _, _, s2, n2 = lagged(m, u, 0)
                if live(m, k):
                    if late(m, n2):
                        sp.wait_ge(L["max_done"], k - 1)
                    for h in range(2):
                        part = negd[ds(h * HALF + k * CH, CH)].rearrange("(a e) -> a e", a=1)
                        sp.dma_start(neg[s2][h * D:(h + 1) * D, 0:CH], part.to_broadcast([D, CH])).then_inc(L[f"neg_loaded_{s2}"], 16)

            run_steps(sp, 0, lambda m, u: load_flags(layers[0], m, u))

            with sp.Fori(0, NG) as g:
                sp.wait_ge(layers[0]["h_ready"], g + 1)
                sp.dma_start(htab[ds(g * (GT * P), GT * P), :].rearrange("(t p) c -> p t c", p=P),
                             hs[:, ds(g * GT, GT), :]).then_inc(layers[0]["h_stored"], 16)

            def load_edges(m, u):
                load_flags(layers[1], m, u)
                k, _, _, s2, n2 = lagged(m, u, 0)
                if live(m, k):
                    if late(m, n2):
                        sp.wait_ge(s_edT, k - 1)
                    by_half = ed[s2].rearrange("p (i h c) -> p i h c", i=TPC, h=2)
                    for h in range(2):
                        left = E - HALF - k * CH if h and isinstance(m, int) else CH
                        whole, rest = min(max(left, 0), CH) // P, min(max(left, 0), CH) % P
                        if whole:
                            sp.dma_start(by_half[:, 0:whole, h, :], edge_attr[ds(h * HALF + k * CH, whole * P), :].rearrange(
                                "(i p) c -> p i c", p=P)).then_inc(s_ed[s2], 16)
                        if rest:
                            sp.dma_start(by_half[0:rest, whole, h, :], edge_attr[E - rest:E, :]).then_inc(s_ed[s2], 16)

            sp.wait_ge(s_u, NCH * SPC)
            run_steps(sp, 0, load_edges)

            for g in range(NG):
                sp.wait_ge(layers[1]["rows_done"], g + 1)
                full = min(GT, (N - g * GT * P) // P)
                sp.dma_start(out[g * GT * P:(g * GT + full) * P, :].rearrange("(t p) c -> p t c", p=P),
                             hs[:, g * GT:g * GT + full, :]).then_inc(s_out, 16)
            rest = N % P
            sp.dma_start(out[N - rest:N, :], hs[0:rest, NT - 1, :]).then_inc(s_out, 16)
            sp.wait_ge(s_out, 16 * (NG + 1))

        @block.gpsimd
        def _(g):
            g.memset(xs[:, NT - 1, :], 0.0).then_inc(s_const, 1)
            g.memset(W1b[:, :], 0.0).then_inc(s_const, 1)
            g.memset(W2b[:, :], 0.0).then_inc(s_const, 1)
            g.memset(drow, N).then_inc(s_const, 1)
            g.wait_ge(s_const, 4)
            g.memset(drow[0:1, 0:1], -1).then_inc(s_const, 1)
            g.memset(ident[:, :], 0.0).then_inc(s_const, 1)
            g.wait_ge(s_const, 6)
            g.affine_select(out=ident[:, :], in_=ident[:, :], compare_op=ALU.not_equal, fill=1.0,
                            base=0, pattern=[[-1, P]], channel_multiplier=1).then_inc(s_const, 1)
            g.iota(iota_i[:, :], pattern=[[1, P]], base=0, channel_multiplier=0).then_inc(s_const, 1)
            for t, value in ((ones[:, :], 1.0), (BD[:, :], 0.0), (bndM[:, :], -BIG), (neg[0][:, CH:CH + 1], 0.0),
                             (neg[1][:, CH:CH + 1], 0.0), (acc[1][:, :], 0.0)):
                g.memset(t, value).then_inc(s_const, 1)

            def gather(L, tab, zz, m, u):
                k, s4, n4, _, _ = lagged(m, u, 0)
                if not live(m, k):
                    return
                g.wait_ge(L["ix_ready"], k + 1)
                if late(m, n4):
                    g.wait_ge(L["sum_done"] if zz is z0 else s_y, k - 3)
                apart(g)
                for s in range(SPC):
                    w = XW if zz is z0 else D
                    g.indirect_dma_start(zz[s4][:, s, 0:w], None, tab[:, :],
                                         bass.IndirectOffsetOnAxis(ap=ixb[s4][:, s:s + 1], axis=0)
                                         ).then_inc(L[f"z_loaded_{s4}"], 16)

            g.wait_ge(s_xtd, 16)
            run_steps(g, 0, lambda m, u: gather(layers[0], xtab, z0, m, u))
            def merge(L, t, rows_):
                if t < NG:
                    if t >= 2:
                        g.wait_ge(L["n_product"], t - 1)
                    cols = slice(t * GT * P, (t + 1) * GT * P)
                    g.tensor_tensor(merged[t % 2][0:rows_, :], acc[0][0:rows_, cols], acc[1][0:rows_, cols], ALU.add).then_inc(L["merged"], 1)

            L = layers[0]
            g.wait_ge(L["join_done"], 1)
            merge(L, 0, D + 1)
            merge(L, 1, D + 1)
            for t in range(NG):
                g.wait_ge(L["xn_ready"], t + 1)
                if t >= 2:
                    g.wait_ge(L["centred"], t - 1)
                g.tensor_tensor(v3(summed[t % 2]), v3(share[t % 2]), xs[:, t * GT:(t + 1) * GT, :], ALU.add).then_inc(L["sum_ready"], 1)
                merge(L, t + 2, D + 1)
            g.wait_ge(L["merged"], NG)
            g.memset(acc[1][:, :], 0.0).then_inc(L["rows_done"], 1)
            g.wait_ge(L["h_stored"], 16 * NG)
            run_steps(g, 0, lambda m, u: gather(layers[1], htab, z1, m, u))
            g.wait_ge(layers[1]["join_done"], 1)
            for t in range(NG):
                merge(layers[1], t, P)

        @block.scalar
        def _(act):
            chain = Chain(act, s_act)
            for q in range(-(-NPAD // 512)):
                w = min(512, NPAD - q * 512)
                act.wait_ge(s_xT, q + 1)
                act.activation(xT[0:D, q * 512:q * 512 + w], bank(4 + q % 4, 0, w)[0:D, :], ACT.Copy).then_inc(s_xTs, 1)
            for q in range(-(-NPAD // 512)):
                w = min(512, NPAD - q * 512)
                act.wait_ge(s_sd, q + 1)
                act.activation(sdst[:, q * 512:q * 512 + w], bank(4 + q % 2, 0, w), ACT.Copy, scale=0.125).then_inc(s_sds, 1)

            def copy_params(L, m, u):
                k, s4, n4, _, _ = lagged(m, u, 0)
                if live(m, k):
                    if late(m, n4):
                        act.wait_ge(L[f"z_loaded_{s4}"], n4 * (16 * SPC))
                        act.wait_ge(L["onehot_ready"], (k - 3) * SPC)
                    act.activation(ixb[s4][:, :], table(srcT, k), ACT.Copy).then_inc(L["ix_ready"], 1)
                    act.activation(relb[s4][:, :], table(relT, k), ACT.Copy).then_inc(L["rel_ready"], 1)
                    act.activation(relc[s4][:, :], table(relC, k), ACT.Copy).then_inc(L["rel_ready"], 1)

            def exp_fac(L, m, u, lag):
                k, _, _, s2, n2 = lagged(m, u, lag)
                if live(m, k):
                    act.wait_ge(L["fac_product"], k + 1)
                    if late(m, n2):
                        act.wait_ge(L["acc_done"], (k - 1) * SPC)
                    act.activation(fac[:, 2 * s2:2 * s2 + 2], bank(7, 0, 2), ACT.Exp,
                                   scale=-1.0).then_inc(L["fac_ready"], 1)

            def step0(m, u):
                L = layers[0]
                copy_params(L, m, u)
                k, _, _, s2, n2 = lagged(m, u, 3)
                if live(m, k):
                    act.wait_ge(s_pd, k + 1)
                    if late(m, n2):
                        act.wait_ge(L["onehot_ready"], (k - 1) * SPC)
                    act.activation(pe_[:, s2 * SPC:(s2 + 1) * SPC], pd[:, s2 * SPC:(s2 + 1) * SPC], ACT.Exp).then_inc(s_p, 1)
                exp_fac(L, m, u, 3)
                k, _, _, s2, _ = lagged(m, u, 2)
                if live(m, k):
                    act.wait_ge(s_e, k + 1)
                    if late(m, k):
                        act.wait_ge(s_et, k)
                    act.activation(eb.rearrange("p (s c) -> p s c", c=D),
                                   es[:, s2 * SPC:(s2 + 1) * SPC].unsqueeze(2).to_broadcast([P, SPC, D]),
                                   ACT.Copy).then_inc(s_eb, 1)

            act.wait_ge(s_tab, 4)
            run_steps(act, 3, step0)

            def join_exp(L):
                act.wait_ge(L["join_ready"], 1)
                act.activation(join[:, 6:8], join[:, 4:6], ACT.Exp).then_inc(L["join_exp"], 1)

            def square_and_root(L, t):
                act.wait_ge(L["centred"], t + 1)
                if t >= 2:
                    act.wait_ge(L["var_ready"], t - 1)
                act.activation(square[t % 2], ybuf[t % 2], ACT.Square).then_inc(L["squared"], 1)
                act.wait_ge(L["var_ready"], t + 1)
                act.activation(small[t % 2][:, 4 * GT:5 * GT], small[t % 2][:, 3 * GT:4 * GT], ACT.Sqrt).then_inc(L["std_ready"], 1)

            L = layers[0]
            join_exp(L)
            for t in range(NG + 1):
                if t < NG:
                    act.wait_ge(L["prodT"], t + 1)
                    if t:
                        act.wait_ge(L["w2_product"], t)
                    act.activation(prodT[0:D, :], ps[0:D, 2 * 512:2 * 512 + GT * P], ACT.Copy).then_inc(L["prodTs"], 1)
                q = t - 1
                if q < 0:
                    continue
                square_and_root(L, q)
                act.wait_ge(L["x1T"], q + 1)
                if q:
                    act.wait_ge(L["h_product"], q)
                act.activation(x1T[:, :], ps[0:D, 2 * 512:2 * 512 + GT * P], ACT.Copy).then_inc(L["x1Ts"], 1)
                act.activation(xs[:, q * GT:(q + 1) * GT, :], v3(x1b[q % 2]), ACT.Copy).then_inc(L["x1_kept"], 1)
                act.wait_ge(L["h_product"], q + 1)
                both = ps[:, 6 * 512:6 * 512 + GT * P].rearrange("p (t c) -> p t c", c=P)
                act.activation(hs[:, q * GT:(q + 1) * GT, :], both[:, :, 0:D], ACT.Copy).then_inc(L["h_ready"], 1)
                act.activation(hl[:, q * GT:(q + 1) * GT, :], both[:, :, D:P], ACT.Copy).then_inc(L["hl_ready"], 1)

            def step1(m, u):
                L = layers[1]
                copy_params(L, m, u)
                k, _, _, s2, n2 = lagged(m, u, 2)
                if live(m, k):
                    act.wait_ge(s_exT, k + 1)
                    if late(m, n2):
                        act.wait_ge(L["sum_done"], k - 1)
                    act.activation(V[s2][:, :, D:P], bank(4).rearrange("p (s c) -> p s c", c=D), ACT.Copy).then_inc(s_den, 1)
                exp_fac(L, m, u, 2)
                k, _, _, s2, n2 = lagged(m, u, 0)
                if live(m, k):
                    act.wait_ge(s_edT, k + 1)
                    if late(m, n2):
                        act.wait_ge(s_ehe, k - 1)
                    act.activation(edT[s2], bank(0), ACT.Copy).then_inc(s_edTs, 1)
                k, _, _, s2, n2 = lagged(m, u, 1)
                if live(m, k):
                    act.wait_ge(s_xsub, k + 1)
                    if late(m, n2):
                        act.wait_ge(s_exT, k - 1)
                    act.activation(Ex[s2], Xs, ACT.Exp).then_inc(s_ex, 1)

            run_steps(act, 3, step1)
            L = layers[1]
            join_exp(L)
            for t in range(NG):
                square_and_root(L, t)

        @block.tensor
        def _(pe):
            pe.wait_ge(s_const, NCONST)
            pe.wait_ge(s_x, 32)
            for q in range(-(-NPAD // 512)):
                if q >= 4:
                    pe.wait_ge(s_xTs, q - 3)
                for t in range(4 * q, min(4 * q + 4, NT)):
                    last = pe.transpose(bank(4 + q % 4, (t % 4) * P, (t % 4 + 1) * P)[0:D, :], xs[:, t, :], ident[:, :])
                last.then_inc(s_xT, 1)
            pe.wait_ge(s_w, 16 * 12)
            for i, w in enumerate((wW1, wW2, wWfc)):
                pe.transpose(bank(0, i * D, (i + 1) * D)[0:D, :], w, ident[0:D, 0:D])
            pe.transpose(bank(0, 3 * D, 4 * D), wWfcr, ident[0:D, 0:D])
            pe.matmul(bank(0, 5 * D, 6 * D)[0:D, :], wWfc, loopS[:, :], start=True, stop=True)
            pe.matmul(bank(0, 4 * D, 4 * D + 2)[0:D + 1, :], wAtt, wa, start=True, stop=True).then_inc(s_wT, 1)
            pe.wait_ge(s_wS, 1)
            for n in range(3):
                pe.wait_ge(s_rowf, n + 1)
                for b in range(BLK):
                    q = min(P, T - b * P)
                    last = pe.transpose(ps[:, b * P:b * P + q], rowf[0:q, b, :], ident[0:q, 0:q])
                last.then_inc(s_rowT, 1)
                if n == 0:
                    pe.wait_ge(s_tab, 1)
                    pe.wait_ge(s_xTs, -(-NPAD // 512))
                    for b in range(-(-T // 512)):
                        w = min(512, T - b * 512)
                        last = pe.matmul(bank(4 + b, 0, w), ones[0:1, :], dT[0:1, b * 512:b * 512 + w], start=True, stop=True)
                    last.then_inc(s_bc, 1)
                    pe.wait_ge(s_tab, 2)
                else:
                    pe.wait_ge(s_tab, n + 2)
            for t in range(NT):
                last = pe.matmul(bank(6, 2 * t, 2 * t + 2), xT[0:D + 1, t * P:(t + 1) * P], vc[:, :], start=True, stop=True)
            last.then_inc(s_sps, 1)
            for q in range(-(-NPAD // 512)):
                w = min(512, NPAD - q * 512)
                if q >= 2:
                    pe.wait_ge(s_sds, q - 1)
                pe.matmul(bank(4 + q % 2, 0, w), vc[:, 1:2].to_broadcast([D + 1, P]), xT[0:D + 1, q * 512:q * 512 + w],
                          start=True, stop=True).then_inc(s_sd, 1)

            def fac_products(L, m, u, lag):
                k, _, _, s2, n2 = lagged(m, u, lag)
                if live(m, k):
                    pe.wait_ge(L["drop_ready"], k + 1)
                    if late(m, k):
                        pe.wait_ge(L["fac_ready"], k)
                    for h in range(2):
                        last = pe.matmul(bank(7, h, h + 1), pick[:, h, :], drop[:, s2:s2 + 1], start=True, stop=True)
                    last.then_inc(L["fac_product"], 1)

            def sums(L, m, u, lag, lhs, slots, rows_):
                k, s4, _, s2, _ = lagged(m, u, lag)
                if live(m, k):
                    pe.wait_ge(L["onehot_ready"], (k + 1) * SPC)
                    if late(m, k):
                        pe.wait_ge(L["acc_done"], k * SPC)
                    b = s4 if slots == 4 else s2
                    apart(pe)
                    reach, = chunk_meta(pe, k, 1)
                    with pe.If(reach < NW):
                        for s in range(SPC):
                            last = pe.matmul(bank(5 + s % 2, 0, NW)[0:rows_, :], lhs[b][:, s, 0:rows_],
                                             oh[s2][:, s, 0:NW], start=s < 2, stop=s >= SPC - 2)
                        last.then_inc(L["sum_done"], 1)
                    with pe.Else():
                        for s in range(SPC):
                            last = pe.matmul(bank(5 + s % 2, s // 2 * P, (s // 2 + 1) * P)[0:rows_, :], lhs[b][:, s, 0:rows_],
                                             oh[s2][:, s, :], start=True, stop=True)
                        last.then_inc(L["sum_done"], 1)

            def step0(m, u):
                L = layers[0]
                k, _, _, s2, _ = lagged(m, u, 2)
                if live(m, k):
                    pe.wait_ge(s_eb, k + 1)
                    if late(m, k):
                        pe.wait_ge(L["fwd_done"], k)
                    for i in range(TPC):
                        last = pe.matmul(bank(0, i * P, (i + 1) * P), eb[:, i * P:(i + 1) * P], ident[:, :], start=True, stop=True)
                    last.then_inc(s_et, 1)
                sums(L, m, u, 3, z0, 4, D + 1)
                k, _, _, s2, _ = lagged(m, u, 2)
                if live(m, k):
                    pe.wait_ge(L["max_done"], k + 1)
                    if late(m, k - 1):
                        pe.wait_ge(s_pd, k - 1)
                    for i in range(TPC):
                        last = pe.matmul(bank(2 + s2, 2 * i, 2 * i + 2), M[s2][:, i * P:(i + 1) * P],
                                         ident[:, 0:P:D], start=True, stop=True)
                    last.then_inc(s_mt, 1)
                fac_products(L, m, u, 2)

            pe.wait_ge(s_tab, 5)
            run_steps(pe, 3, step0)

            def join_products(L):
                pe.wait_ge(L["bnd_done"], NCH)
                pe.wait_ge(L["fac_ready"], NCH)
                pe.matmul(bank(7, 100, 101), pick[:, 0, :], F[(NCH - 1) % 2][:, CH - 1:CH], start=True, stop=True)
                pe.matmul(bank(7, 101, 102), pick[:, 1, :], bndM[:, (NCH - 1) % 2:(NCH - 1) % 2 + 1], start=True, stop=True).then_inc(L["join_product"], 1)

            L = layers[0]
            join_products(L)

            def n_products(t):
                pe.wait_ge(L["merged"], t + 1)
                if t >= 2:
                    pe.wait_ge(L["xn_ready"], t - 1)
                for i in range(GT):
                    last = pe.matmul(bank(t % 2, i * (D + 1), (i + 1) * (D + 1)), merged[t % 2][0:D + 1, i * P:(i + 1) * P], W1b[:, :],
                                     start=True, stop=True)
                last.then_inc(L["n_product"], 1)

            n_products(0)
            for t in range(NG + 1):
                if t < NG:
                    pe.wait_ge(L["xn_ready"], t + 1)
                    if t >= 2:
                        pe.wait_ge(L["x1Ts"], t - 1)
                    for i in range(GT):
                        last = pe.transpose(ps[0:D, 2 * 512 + i * P:2 * 512 + (i + 1) * P], prod[t % 2][:, i * D:(i + 1) * D], ident[:, :])
                    last.then_inc(L["prodT"], 1)
                    if t + 1 < NG:
                        n_products(t + 1)
                    pe.wait_ge(L["prodTs"], t + 1)
                    if t >= 2:
                        pe.wait_ge(L["centred"], t - 1)
                    for i in range(GT):
                        last = pe.matmul(bank(4 + t % 2, i * D, (i + 1) * D), prodT[:, i * P:(i + 1) * P], W2b[:, :], start=True, stop=True)
                    last.then_inc(L["w2_product"], 1)
                q = t - 1
                if q < 0:
                    continue
                pe.wait_ge(L["x1_ready"], q + 1)
                for i in range(GT):
                    last = pe.transpose(ps[0:D, 2 * 512 + i * P:2 * 512 + (i + 1) * P], x1b[q % 2][:, i * D:(i + 1) * D], ident[:, :])
                last.then_inc(L["x1T"], 1)
                pe.wait_ge(L["x1Ts"], q + 1)
                if q:
                    pe.wait_ge(L["hl_ready"], q)
                for i in range(GT):
                    last = pe.matmul(ps[:, 6 * 512 + i * P:6 * 512 + (i + 1) * P], x1T[:, i * P:(i + 1) * P], WH[:, :], start=True, stop=True)
                last.then_inc(L["h_product"], 1)

            def step1(m, u):
                L = layers[1]
                k, _, _, s2, n2 = lagged(m, u, 1)
                if live(m, k):
                    pe.wait_ge(s_edTs, k + 1)
                    if late(m, k):
                        pe.wait_ge(s_xsub, k)
                    pe.matmul(bank(1), BD[:, :], edT[s2], start=True, stop=True).then_inc(s_eh, 1)
                k, _, _, s2, _ = lagged(m, u, 2)
                if live(m, k):
                    pe.wait_ge(s_ex, k + 1)
                    if late(m, k):
                        pe.wait_ge(s_den, k)
                    for i in range(TPC):
                        last = pe.transpose(bank(4, i * P, (i + 1) * P), Ex[s2][:, i * P:(i + 1) * P], ident[:, :])
                    last.then_inc(s_exT, 1)
                fac_products(L, m, u, 2)
                k, _, _, s2, n2 = lagged(m, u, 0)
                if live(m, k):
                    pe.wait_ge(s_ed[s2], n2 * 32 + 16 * edge_loads(m, k))
                    if late(m, k):
                        pe.wait_ge(s_edTs, k)
                    for i in range(TPC):
                        last = pe.transpose(bank(0, i * P, (i + 1) * P), ed[s2][:, i * P:(i + 1) * P], ident[:, :])
                    last.then_inc(s_edT, 1)
                k, _, _, s2, n2 = lagged(m, u, 1)
                if live(m, k):
                    if late(m, n2):
                        pe.wait_ge(s_y, k - 1)
                    for i in range(TPC):
                        last = pe.matmul(bank(2 + s2, i * P, (i + 1) * P), edT[s2][:, i * P:(i + 1) * P], BD[:, :], start=True, stop=True)
                    last.then_inc(s_ehe, 1)
                k, _, _, s2, n2 = lagged(m, u, 3)
                if live(m, k):
                    pe.wait_ge(s_val, k + 1)
                sums(L, m, u, 3, V, 2, P)

            pe.wait_ge(layers[0]["layer_done"], 1)
            run_steps(pe, 3, step1)
            L = layers[1]
            join_products(L)
            for t in range(NG):
                pe.wait_ge(L["merged"], t + 1)
                if t >= 2:
                    pe.wait_ge(L["sum_ready"], t - 1)
                for i in range(GT):
                    last = pe.transpose(ps[:, t % 2 * 1024 + i * P:t % 2 * 1024 + (i + 1) * P], merged[t % 2][:, i * P:(i + 1) * P], ident[:, :])
                last.then_inc(L["n_product"], 1)

        @block.vector
        def _(dve):
            chain = Chain(dve, s_dve)
            dve.wait_ge(s_const, NCONST)
            dve.memset(prodT[D:D + 1, :], 1.0)
            dve.tensor_copy(iota[:, :], iota_i[:, :])
            for h in range(2):
                dve.tensor_copy(pick[:, h, :].rearrange("p (a c) -> p a c", a=2),
                                ident[:, h * D:(h + 1) * D].unsqueeze(1).to_broadcast([P, 2, D]))
            dve.memset(rows[:, BLK - 1, :], N).then_inc(s_pads, 1)
            dve.wait_ge(s_drow, 16 * 5)
            rf = rowf.rearrange("p b j -> p (b j)")[:, 0:T]
            chain(dve.tensor_tensor(rf, drow[:, 1:T + 1], drow[:, 0:T], ALU.not_equal))
            chain(dve.tensor_scalar(negs, rf, -BIG, None, ALU.mult))
            dve.sem_inc(s_negs, 1)
            dve.wait_ge(s_wT, 1)
            dve.tensor_copy(W1b[0:D, 0:D], bank(0, 0, D)[0:D, :])
            dve.memset(W1b[D:D + 1, D:D + 1], 1.0)
            dve.tensor_copy(W2b[0:D, :], bank(0, D, 2 * D)[0:D, :])
            dve.tensor_copy(WH[:, 0:D], bank(0, 2 * D, 3 * D)[0:D, :])
            dve.tensor_copy(WH[:, D:P], bank(0, 5 * D, 6 * D)[0:D, :])
            dve.tensor_copy(BD[0:D, 0:D], bank(0, 3 * D, 4 * D)[0:D, :])
            dve.tensor_copy(BD[D:P, D:P], bank(0, 3 * D, 4 * D)[D:P, :])
            chain(dve.tensor_copy(vc[:, :], bank(0, 4 * D, 4 * D + 2)[0:D + 1, :]))
            dve.memset(xT[D:D + 1, 0:NPAD], 1.0).then_inc(s_wS, 1)

            metas = meta[:, :].rearrange("p (k n) -> p k n", n=META)

            def halves(t):
                return [t.rearrange("p (t h) -> p h t", h=2)[:, h, :] for h in range(2)]

            for n in range(3):
                dve.wait_ge(s_rows, 48 * (n + 1))
                chain(dve.tensor_copy(rowf, rows))
                dve.sem_inc(s_rowf, 1)
                if n < 2:
                    dve.memset(rows[:, BLK - 1, :], 1 - n).then_inc(s_pads, 1)
                dve.wait_ge(s_rowT, n + 1)
                if n == 0:
                    chain(dve.tensor_copy(dT, ps[:, 0:T]))
                    dve.sem_inc(s_tab, 1)
                    dve.wait_ge(s_bc, 1)
                    for h in range(2):
                        dve.tensor_tensor(halves(relT)[h], dT[:, h * HT:(h + 1) * HT],
                                          ps[:, 2048 + h * HT:2048 + (h + 1) * HT], ALU.subtract)
                        first = ps[:, 2048 + h * HT:2048 + (h + 1) * HT:TPC]
                        dve.tensor_tensor(halves(relC)[h].rearrange("p (k i) -> p k i", i=TPC),
                                          dT[:, h * HT:(h + 1) * HT].rearrange("p (k i) -> p k i", i=TPC),
                                          first.unsqueeze(2).to_broadcast([P, NCH, TPC]), ALU.subtract)
                        row = dT[0:1, h * HT:(h + 1) * HT].rearrange("p (k i) -> p k i", i=TPC)
                        dve.tensor_copy(metas[:, :, 1:1 + SPC].rearrange("p k (i h) -> p h k i", h=2)[:, h, :, :], row)
                        nxt = dT[0:1, (h + 1) * HT - (NCH - 1) * TPC:(h + 1) * HT:TPC] if h else dT[0:1, TPC:HT + 1:TPC]
                        n_next = NCH - h
                        dve.tensor_tensor(reach2[:, h, 0:n_next], nxt, dT[0:1, h * HT:h * HT + (n_next - 1) * TPC + 1:TPC], ALU.subtract)
                    dve.tensor_scalar(reach2[:, 1, NCH - 1:NCH], dT[0:1, T - TPC:T - TPC + 1], -1.0, float(N), ALU.mult, ALU.add)
                    chain(dve.tensor_copy(join[:, 0:1], ps[:, 2048 + HT:2048 + HT + 1]))
                    chain(dve.tensor_tensor(metas[:, :, 0], reach2[:, 0, :], reach2[:, 1, :], ALU.max))
                    chain(dve.tensor_scalar(bnd[:, :], ps[:, 2048 + HT:2048 + T:TPC], join[:, 0:1], -BIG,
                                            ALU.not_equal, ALU.mult))
                elif n == 1:
                    for h in range(2):
                        last = dve.tensor_scalar(halves(biasT)[h], ps[:, h * HT:(h + 1) * HT], 0.0, 0.625, ALU.is_equal, ALU.mult)
                    chain(last)
                else:
                    for h in range(2):
                        last = dve.tensor_copy(halves(srcT)[h], ps[:, h * HT:(h + 1) * HT])
                    chain(last)
                dve.sem_inc(s_tab, 1)
            dve.wait_ge(s_x, 32)
            dve.tensor_copy(xtb[:, :, 0:D], xs[:, :, :])
            dve.memset(xtb[:, :, D:D + 1], 1.0)
            dve.wait_ge(s_sps, 1)
            chain(dve.tensor_scalar(xtb[:, :, D + 1:D + 2], bank(6, 0, 2 * NT).rearrange("p (t c) -> p t c", c=2)[:, :, 0:1],
                                    0.125, None, ALU.mult))
            dve.sem_inc(s_xtb, 1)
            dve.wait_ge(s_sds, -(-NPAD // 512))
            dve.memset(sdst[:, NPAD:ACCW], 0.0)
            chain(dve.memset(acc[0][:, :], 0.0))
            dve.sem_inc(s_tab, 1)
            dve.wait_ge(s_cont, 16)

            def scans(L, m, u, lag, scores):
                k, _, _, s2, n2 = lagged(m, u, lag)
                dve.wait_ge(L[f"neg_loaded_{s2}"], (n2 + 1) * 32)
                first = -BIG if isinstance(k, int) and k == 0 else F[1 - s2][:, CH - 1:CH]
                if late(m, k - 1):
                    dve.wait_ge(L["bnd_done"], k)
                dve.tensor_tensor_scan(F[s2], neg[s2][:, 0:CH], scores, first, ALU.add, ALU.max).then_inc(L["fwd_done"], 1)
                dve.wait_ge(L["fwd_done"], k + 1)
                dve.tensor_tensor_scan(M[s2][:, ::-1], neg[s2][:, CH:0:-1], F[s2][:, ::-1], F[s2][:, CH - 1:CH],
                                       ALU.add, ALU.max).then_inc(L["max_done"], 1)
                dve.wait_ge(L["max_done"], k + 1)
                prev = -BIG if isinstance(k, int) and k == 0 else F[1 - s2][:, CH - 1:CH]
                if late(m, n2):
                    dve.wait_ge(L["fac_product"], k - 1)
                if isinstance(k, int) and k == 0:
                    dve.memset(drop[:, 0:1], 0.0).then_inc(L["drop_ready"], 1)
                else:
                    dve.tensor_scalar(drop[:, s2:s2 + 1], M[s2][:, 0:1], prev, 0.0, ALU.subtract, ALU.max).then_inc(L["drop_ready"], 1)
                dve.scalar_tensor_tensor(bndM[:, s2:s2 + 1], M[s2][:, 0:1], bnd[:, ds(k, 1)], bndM[:, 1 - s2:2 - s2],
                                         ALU.add, ALU.max).then_inc(L["bnd_done"], 1)

            def add_windows(L, m, u, lag, rows_):
                k, _, _, s2, _ = lagged(m, u, lag)
                if not live(m, k):
                    return
                dve.wait_ge(L["sum_done"], k + 1)
                dve.wait_ge(L["fac_ready"], k + 1)
                apart(dve)
                reach, *at_ = chunk_meta(dve, k, 1 + SPC)
                with dve.If(reach < NW):
                    if late(m, k):
                        dve.wait_ge(L["acc_done"], k * SPC)
                    for h in range(2):
                        win = acc[h][0:rows_, ds(at_[h], NW)]
                        dve.scalar_tensor_tensor(win, win, fac[0:rows_, 2 * s2 + h:2 * s2 + h + 1], bank(5 + h, 0, NW)[0:rows_, :],
                                                 ALU.mult, ALU.add).then_inc(L["acc_done"], TPC)
                with dve.Else():
                    for s in range(SPC):
                        h = s % 2
                        win = acc[h][0:rows_, ds(at_[s], P)]
                        new = bank(5 + h, s // 2 * P, (s // 2 + 1) * P)[0:rows_, :]
                        if not (isinstance(k, int) and k == 0 and s < 2):
                            dve.wait_ge(L["acc_done"], k * SPC + s - 1)
                        if s < 2:
                            dve.scalar_tensor_tensor(win, win, fac[0:rows_, 2 * s2 + h:2 * s2 + h + 1], new,
                                                     ALU.mult, ALU.add).then_inc(L["acc_done"], 1)
                        else:
                            dve.tensor_tensor(win, win, new, ALU.add).then_inc(L["acc_done"], 1)

            def step0(m, u):
                L = layers[0]
                k, _, _, s2, n2 = lagged(m, u, 3)
                sl = slice(s2 * SPC, (s2 + 1) * SPC)
                if live(m, k):
                    dve.wait_ge(s_mt, k + 1)
                    if late(m, n2):
                        dve.wait_ge(s_p, k - 1)
                    dve.tensor_tensor(pd[:, sl], es[:, sl], bank(2 + s2, 0, SPC), ALU.subtract).then_inc(s_pd, 1)
                k, s4, n4, s2, n2 = lagged(m, u, 2)
                sl = slice(s2 * SPC, (s2 + 1) * SPC)
                if live(m, k):
                    dve.wait_ge(L[f"z_loaded_{s4}"], (n4 + 1) * (16 * SPC))
                    dve.wait_ge(s_u, (k + 1) * SPC)
                    dve.tensor_tensor(ts[:, sl], us[:, sl], z0[s4][:, :, D + 1], ALU.add).then_inc(s_t, 1)
                    dve.wait_ge(s_t, 2 * k + 1)
                    dve.tensor_tensor(ubb[:, sl], ts[:, sl], table(biasT, k), ALU.add).then_inc(s_t, 1)
                    dve.wait_ge(s_t, 2 * k + 2)
                    if late(m, n2):
                        dve.wait_ge(s_pd, k - 1)
                    dve.scalar_tensor_tensor(es[:, sl], ubb[:, sl], 0.2, ubb[:, sl], ALU.mult, ALU.max).then_inc(s_e, 1)
                k, s4, _, s2, n2 = lagged(m, u, 3)
                if live(m, k):
                    dve.wait_ge(s_p, k + 1)
                    if late(m, n2):
                        dve.wait_ge(L["sum_done"], k - 1)
                    apart(dve)
                    reach, = chunk_meta(dve, k, 1)
                    with dve.If(reach < NW):
                        dve.tensor_tensor(oh[s2][:, :, 0:NW], ohn[s4], pe_[:, s2 * SPC:(s2 + 1) * SPC].unsqueeze(2).to_broadcast([P, SPC, NW]),
                                          ALU.mult).then_inc(L["onehot_ready"], SPC)
                    with dve.Else():
                        for s in range(SPC):
                            dve.tensor_scalar(oh[s2][:, s, :], iota[:, :], relb[s4][:, s:s + 1],
                                              pe_[:, s2 * SPC + s:s2 * SPC + s + 1], ALU.is_equal, ALU.mult).then_inc(L["onehot_ready"], 1)
                k, s4, _, s2, _ = lagged(m, u, 1)
                if live(m, k):
                    dve.wait_ge(L["rel_ready"], 2 * k + 2)
                    apart(dve)
                    reach, *at_ = chunk_meta(dve, k, 1 + SPC)
                    mine = us[:, s2 * SPC:(s2 + 1) * SPC]
                    with dve.If(reach < NW):
                        dve.tensor_tensor(ohn[s4], iota[:, 0:NW].unsqueeze(1).to_broadcast([P, SPC, NW]),
                                          relc[s4][:, :].unsqueeze(2).to_broadcast([P, SPC, NW]), ALU.is_equal).then_inc(s_u, 1)
                        dve.wait_ge(s_u, k * SPC + 1)
                        both = junk.rearrange("p (i h w) -> p h i w", h=2, w=NW)
                        for h in range(2):
                            dve.tensor_tensor(both[:, h, :, :], ohn[s4].rearrange("p (i h) w -> p h i w", h=2)[:, h, :, :],
                                              sdst[:, ds(at_[h], NW)].unsqueeze(1).to_broadcast([P, TPC, NW]), ALU.mult).then_inc(s_u, 1)
                        dve.wait_ge(s_u, k * SPC + 3)
                        dve.tensor_reduce(mine, junk.rearrange("p (s w) -> p s w", w=NW), AX.X, ALU.add).then_inc(s_u, SPC - 3)
                    with dve.Else():
                        for s in range(SPC):
                            if not (isinstance(k, int) and k == 0 and s < 2):
                                dve.wait_ge(s_u, k * SPC + s - 1)
                            dve.scalar_tensor_tensor(junk[:, s % 2 * P:(s % 2 + 1) * P], iota[:, :], relb[s4][:, s:s + 1],
                                                     sdst[:, ds(at_[s], P)], ALU.is_equal, ALU.mult,
                                                     accum_out=mine[:, s:s + 1]).then_inc(s_u, 1)
                k, _, _, s2, _ = lagged(m, u, 2)
                if live(m, k):
                    dve.wait_ge(s_et, k + 1)
                    if late(m, k - 1):
                        dve.wait_ge(s_mt, k - 1)
                    scans(L, m, u, 2, bank(0))
                add_windows(L, m, u, 3, D + 1)

            run_steps(dve, 3, step0)

            def join_halves(L, rows_, chain):
                dve.wait_ge(L["join_product"], 1)
                dve.wait_ge(L["acc_done"], NCH * SPC)
                chain(dve.tensor_copy(join[:, 0:2], bank(7, 100, 102)))
                chain(dve.tensor_tensor(join[:, 2:3], join[:, 0:1], cont[:, 0:1], ALU.add))
                chain(dve.tensor_tensor(join[:, 3:4], join[:, 2:3], join[:, 1:2], ALU.max))
                chain(dve.tensor_tensor(join[:, 4:5], join[:, 2:3], join[:, 3:4], ALU.subtract))
                chain(dve.tensor_tensor(join[:, 5:6], join[:, 1:2], join[:, 3:4], ALU.subtract))
                dve.sem_inc(L["join_ready"], 1)
                dve.wait_ge(L["join_exp"], 1)
                apart(dve)
                at_ = chunk_meta(dve, 0, 3)[2:]
                for h in range(2):
                    one = acc[h][0:rows_, ds(at_[0], 1)]
                    chain(dve.tensor_scalar(one, one, join[0:rows_, 6 + h:7 + h], None, ALU.mult))

            def spread(t):
                return t.unsqueeze(2).to_broadcast([P, GT, D])

            def centre(L, chain, t):
                y, sm = ybuf[t % 2], small[t % 2]
                chain(dve.tensor_reduce(sm[:, GT:2 * GT], v3(y), AX.X, ALU.add))
                chain(dve.tensor_scalar(sm[:, GT:2 * GT], sm[:, GT:2 * GT], 1.0 / D, None, ALU.mult))
                dve.tensor_tensor(v3(y), v3(y), spread(sm[:, GT:2 * GT]), ALU.subtract).then_inc(L["centred"], 1)

            def scale(L, chain, t, dest):
                y, sm = ybuf[t % 2], small[t % 2]
                dve.wait_ge(L["squared"], t + 1)
                chain(dve.tensor_reduce(sm[:, 2 * GT:3 * GT], v3(square[t % 2]), AX.X, ALU.add))
                dve.tensor_scalar(sm[:, 3 * GT:4 * GT], sm[:, 2 * GT:3 * GT], 1.0 / D, 1e-5, ALU.mult, ALU.add).then_inc(L["var_ready"], 1)
                dve.wait_ge(L["std_ready"], t + 1)
                chain(dve.reciprocal(sm[:, 4 * GT:5 * GT], sm[:, 4 * GT:5 * GT]))
                return dve.tensor_tensor(dest, v3(y), spread(sm[:, 4 * GT:5 * GT]), ALU.mult)

            L = layers[0]
            chain = Chain(dve, L["dve_epi"])
            join_halves(L, D + 1, chain)
            dve.sem_inc(L["join_done"], 1)
            for t in range(NG + 2):
                if t < NG:
                    xg = xs[:, t * GT:(t + 1) * GT, :]
                    dve.wait_ge(L["n_product"], t + 1)
                    nb = bank(t % 2, 0, GT * (D + 1)).rearrange("p (t c) -> p t c", c=D + 1)
                    rden = small[t % 2][:, 0:GT]
                    dve.tensor_scalar(no_edge[:, t * GT:(t + 1) * GT], nb[:, :, D], 0.0, None, ALU.is_equal)
                    chain(dve.tensor_scalar(rden, nb[:, :, D], 1e-9, None, ALU.add))
                    chain(dve.reciprocal(rden, rden))
                    if t >= 2:
                        dve.wait_ge(L["sum_ready"], t - 1)
                    chain(dve.tensor_tensor(v3(share[t % 2]), nb[:, :, 0:D], spread(rden), ALU.mult))
                    if t >= 2:
                        dve.wait_ge(L["prodT"], t - 1)
                    dve.tensor_tensor(v3(prod[t % 2]), v3(share[t % 2]), xg, ALU.mult).then_inc(L["xn_ready"], 1)
                q = t - 1
                if 0 <= q < NG:
                    y, xg = ybuf[q % 2], xs[:, q * GT:(q + 1) * GT, :]
                    dve.wait_ge(L["w2_product"], q + 1)
                    dve.wait_ge(L["sum_ready"], q + 1)
                    chain(dve.tensor_tensor(y, summed[q % 2], bank(4 + q % 2, 0, GT * D), ALU.add))
                    chain(dve.scalar_tensor_tensor(y, y, 0.2, y, ALU.mult, ALU.max))
                    chain(dve.tensor_tensor(v3(y), v3(y), xg, ALU.add))
                    centre(L, chain, q)
                r = t - 2
                if r >= 0:
                    dve.wait_ge(L["hl_ready"], r + 1)
                    apart(dve)
                    dve.copy_predicated(hl[:, r * GT:(r + 1) * GT, :], spread(no_edge[:, r * GT:(r + 1) * GT].bitcast(u32)),
                                        hs[:, r * GT:(r + 1) * GT, :])
                if 0 <= q < NG:
                    if q >= 2:
                        dve.wait_ge(L["x1_kept"], q - 1)
                    scale(L, chain, q, v3(x1b[q % 2])).then_inc(L["x1_ready"], 1)
            dve.wait_ge(L["merged"], NG)
            dve.memset(acc[0][:, :], 0.0)
            chain(dve.memset(bndM[:, :], -BIG))
            dve.wait_ge(L["rows_done"], 1)
            dve.sem_inc(L["layer_done"], 1)

            def step1(m, u):
                L = layers[1]
                k, _, _, s2, _ = lagged(m, u, 1)
                if live(m, k):
                    dve.wait_ge(s_eh, k + 1)
                    scans(L, m, u, 1, bank(1))
                    if late(m, k):
                        dve.wait_ge(s_ex, k)
                    dve.tensor_tensor(Xs, bank(1), M[s2], ALU.subtract).then_inc(s_xsub, 1)
                k, s4, n4, s2, n2 = lagged(m, u, 2)
                if live(m, k):
                    dve.wait_ge(L[f"z_loaded_{s4}"], (n4 + 1) * (16 * SPC))
                    dve.wait_ge(s_ehe, k + 1)
                    if late(m, k):
                        dve.wait_ge(s_val, k)
                    dve.tensor_tensor(Y, bank(2 + s2), z[s4][:, 0:SPC * D], ALU.add).then_inc(s_y, 1)
                    dve.wait_ge(L["rel_ready"], 2 * k + 2)
                    if late(m, n2):
                        dve.wait_ge(L["sum_done"], k - 1)
                    apart(dve)
                    reach, = chunk_meta(dve, k, 1)
                    with dve.If(reach < NW):
                        dve.tensor_tensor(oh[s2][:, :, 0:NW], iota[:, 0:NW].unsqueeze(1).to_broadcast([P, SPC, NW]),
                                          relc[s4][:, :].unsqueeze(2).to_broadcast([P, SPC, NW]), ALU.is_equal
                                          ).then_inc(L["onehot_ready"], SPC)
                    with dve.Else():
                        for s in range(SPC):
                            dve.tensor_scalar(oh[s2][:, s, :], iota[:, :], relb[s4][:, s:s + 1], None,
                                              ALU.is_equal).then_inc(L["onehot_ready"], 1)
                    dve.wait_ge(s_den, k + 1)
                    dve.wait_ge(s_y, k + 1)
                    dve.tensor_tensor(V[s2][:, :, 0:D], V[s2][:, :, D:P], Y.rearrange("p (s c) -> p s c", c=D),
                                      ALU.mult).then_inc(s_val, 1)
                add_windows(L, m, u, 3, P)

            run_steps(dve, 3, step1)

            L = layers[1]
            chain = Chain(dve, L["dve_epi"])
            join_halves(L, P, chain)
            dve.sem_inc(L["join_done"], 1)
            for t in range(NG + 1):
                if t < NG:
                    rows_ = slice(t * GT, (t + 1) * GT)
                    dve.wait_ge(L["n_product"], t + 1)
                    nb = ps[:, t % 2 * 1024:t % 2 * 1024 + GT * P].rearrange("p (t c) -> p t c", c=P)
                    chain(dve.tensor_scalar(v3(share[0]), nb[:, :, D:P], 1e-30, None, ALU.max))
                    chain(dve.reciprocal(share[0], share[0]))
                    dve.tensor_tensor(v3(prod[0]), nb[:, :, 0:D], v3(share[0]), ALU.mult).then_inc(L["sum_ready"], 1)
                    dve.wait_ge(L["sum_ready"], t + 1)
                    chain(dve.tensor_tensor(v3(prod[0]), v3(prod[0]), hl[:, rows_, :], ALU.add))
                    if t >= 2:
                        dve.wait_ge(L["rows_done"], t - 1)
                    chain(dve.scalar_tensor_tensor(v3(ybuf[t % 2]), v3(prod[0]), 0.0, xs[:, rows_, :], ALU.max, ALU.add))
                    centre(L, chain, t)
                q = t - 1
                if q >= 0:
                    scale(L, chain, q, hs[:, q * GT:(q + 1) * GT, :]).then_inc(L["rows_done"], 1)


_INS = ['x', 'src', 'dst', 'edge_attr_64', 'edge_type_4', 'L0_gnn_W1_w', 'L0_gnn_W1_b', 'L0_gnn_W2_w', 'L0_gnn_W2_b',
        'L0_gnn_W_att_w', 'L0_gnn_W_att_b', 'L0_gnn_a', 'L1_gnn_W_fc', 'L1_gnn_W_fcr', 'L1_gnn_loop_W']
_OUTS = [((N, D), 'float32')]


def kernel(**inputs):
    import numpy as _np
    import concourse.bacc as _bacc
    from concourse import mybir as _mybir
    from concourse.bass_utils import run_bass_kernel_spmd as _run

    nc = _bacc.Bacc("TRN2", target_bir_lowering=False, num_devices=1)
    arrays, args = {}, []
    for name in _INS:
        a = _np.ascontiguousarray(inputs[name])
        arrays[f"in_{name}_dram"] = a
        args.append(nc.dram_tensor(f"in_{name}_dram", a.shape, _mybir.dt.from_np(a.dtype), kind="ExternalInput").ap())
    for i, (shape, dtype) in enumerate(_OUTS):
        dt = _mybir.dt.from_np(_np.dtype(dtype))
        args.append(nc.dram_tensor(f"out_{i}_dram", shape, dt, kind="ExternalOutput").ap())
    gnn_kernel(nc, *args)
    r = _run(nc, [arrays], core_ids=[0])
    got = tuple(r.results[0][f"out_{i}_dram"] for i in range(len(_OUTS)))
    return got[0]
```

```python
import concourse.bass as bass
from concourse import mybir
from contextlib import ExitStack

P = 128
D = 64
N = 6250
E = 206250
TPC = 4
CH = TPC * P
NCH = -(-E // (2 * CH))
HT = NCH * TPC
HALF = HT * P
T = 2 * HT
SPC = 2 * TPC
NT = -(-N // P)
NPAD = NT * P
ACCW = NPAD + P
GT = 7
NG = NT // GT
PAIRS = -(-GT // 2)
XW = D + 2
BIG = float(2.0 ** 100)
NW = 32
META = 12
UNROLL = 4
HEAD = 2 * UNROLL
BLK = -(-T // P)


def lagged(m, u, lag):
    d = u - lag
    return m * UNROLL + d, d % 4, m + d // 4, d % 2, m * 2 + d // 2


def live(m, k):
    return not isinstance(m, int) or 0 <= k < NCH


def late(m, count):
    return not isinstance(m, int) or count > 0


def run_steps(eng, lags, step):
    total = NCH + lags
    loops = (NCH - HEAD) // UNROLL
    for s in range(HEAD):
        step(s // UNROLL, s % UNROLL)
    with eng.Fori(HEAD // UNROLL, HEAD // UNROLL + loops) as m:
        for u in range(UNROLL):
            step(m, u)
    for s in range(HEAD + loops * UNROLL, total):
        step(s // UNROLL, s % UNROLL)


def edge_loads(m, k):
    if not isinstance(m, int):
        return 2
    left = min(max(E - HALF - k * CH, 0), CH)
    return 1 + (left >= P) + (left % P > 0)


def whole_slots(m, k):
    return [s for s in range(SPC) if s % 2 == 0 or not isinstance(m, int) or HALF + k * CH + s // 2 * P < E]


assert HEAD + (NCH - HEAD) // UNROLL * UNROLL <= (E - HALF) // CH


class Chain:

    def __init__(self, eng, sem, base=0):
        self.eng, self.sem, self.base, self.n = eng, sem, base, 0

    def __call__(self, ins):
        ins.then_inc(self.sem, 1)
        self.n += 1
        self.eng.wait_ge(self.sem, self.base + self.n)


def gnn_kernel(nc, x, src, dst, edge_attr, edge_type, W1, b1, W2, b2, Watt, batt, a, Wfc, Wfcr, loopW, out):
    f32, i32, u32, bf16 = mybir.dt.float32, mybir.dt.int32, mybir.dt.uint32, mybir.dt.bfloat16
    ALU, ACT, AX = mybir.AluOpType, mybir.ActivationFunctionType, mybir.AxisListType
    ds = bass.ds

    xtab = nc.dram_tensor("xtab", (NPAD, XW), f32).ap()
    htab = nc.dram_tensor("htab", (NPAD, D), f32).ap()
    negd = nc.dram_tensor("negd", (2 * HALF,), bf16).ap()
    sdd = nc.dram_tensor("sdd", (NPAD,), f32).ap()

    ctx = ExitStack()
    with ctx:
        def sb(name, shape, dt=f32):
            return ctx.enter_context(nc.sbuf_tensor(name, shape, dt))

        def sem(name):
            return ctx.enter_context(nc.semaphore(name))

        srcT = sb("srcT", [P, T], u32)
        relT = sb("relT", [P, T])
        biasT = sb("biasT", [P, T])
        relC = sb("relC", [P, T])
        meta = sb("meta", [1, NCH * META], i32)
        bnd = sb("bnd", [P, NCH])
        acc = [sb("accA", [P, ACCW]), sb("accB", [P, ACCW])]
        xs = sb("xs", [P, NT, D])
        hh = sb("hh", [P, 2, NT * D])
        hs = hh[:, 0, :].rearrange("p (t c) -> p t c", c=D)
        hl = hh[:, 1, :].rearrange("p (t c) -> p t c", c=D)
        xtb = hh[:, :, :].rearrange("p a b -> p (a b)")[:, 0:NT * XW].rearrange("p (t c) -> p t c", c=XW)
        ident = sb("ident", [P, P])
        pick = sb("pick", [P, 2, P])
        iota = sb("iota", [P, P])
        iota_i = sb("iota_i", [P, P], i32)
        ones = sb("ones", [1, P])
        tiny = sb("tiny", [P, 1])
        W1b = sb("W1b", [D + 1, D + 1])
        b2b = sb("b2b", [P, D])
        W2d = sb("W2d", [P, P])
        WHd = sb("WHd", [P, P])
        WLd = sb("WLd", [P, P])
        WRd = sb("WRd", [P, P])
        loopS = sb("loopS", [D, D])
        wl = sb("wl", [D, 8 * D + 1 + 2])
        wW1 = wl[:, 0:D]
        wW2, wWfc, wWfcr = (wl[:, i * D:(i + 2) * D] for i in (1, 3, 5))
        wAtt = wl[:, 7 * D:8 * D + 1]
        wa = wl[:, 8 * D + 1:8 * D + 3]
        bndM = sb("bndM", [P, 2])
        cont = sb("cont", [P, 1], bf16)
        join = sb("join", [P, 8])

        NF = 10752
        arena = sb("arena", [P, NF])
        at = [0]

        def carve(n, dt=f32):
            w = n if dt in (f32, i32, u32) else -(-n // 2)
            ap = arena[:, at[0]:at[0] + w]
            at[0] += w
            assert at[0] <= NF
            return ap if dt == f32 else ap.bitcast(dt)

        ixb = [sb(f"ixb{i}", [P, SPC], u32) for i in range(4)]
        relb = [sb(f"relb{i}", [P, SPC]) for i in range(4)]
        relc = [sb(f"relc{i}", [P, SPC]) for i in range(4)]
        z = [carve(SPC * XW) for _ in range(4)]
        z0 = [t.rearrange("p (s c) -> p s c", c=XW) for t in z]
        z1 = [t[:, 0:SPC * D].rearrange("p (s c) -> p s c", c=D) for t in z]
        neg = [sb(f"neg{i}", [P, CH + 1], bf16) for i in range(2)]
        F = [carve(CH) for _ in range(2)]
        M = [carve(CH) for _ in range(2)]
        oh = [carve(SPC * P).rearrange("p (s w) -> p s w", w=P) for _ in range(2)]
        drop = sb("drop", [P, 2])
        fac = sb("fac", [P, 4])
        us = sb("us", [P, 2 * SPC])
        ts = sb("ts", [P, 2 * SPC])
        ubb = sb("ubb", [P, 2 * SPC])
        es = sb("es", [P, 2 * SPC])
        pd = sb("pd", [P, 2 * SPC])
        pe_ = sb("pe_", [P, 2 * SPC])
        junk = carve(SPC * NW)
        ohn = [carve(SPC * NW).rearrange("p (s w) -> p s w", w=NW) for _ in range(4)]
        eb = carve(CH)
        at[0] = 4 * SPC * XW
        share, summed, ybuf, square = ([carve(GT * D) for _ in range(2)] for _ in range(4))
        prod, x1b = ([carve(PAIRS * P) for _ in range(2)] for _ in range(2))
        no_edge = sb("no_edge", [P, NT])
        merged = [carve(GT * P) for _ in range(2)]
        small = [sb(f"small{i}", [P, 5 * GT]) for i in range(2)]
        prodT = sb("prodT", [P, PAIRS * P])
        big = sb("big", [P, ACCW])
        sdst = big
        xp = big[:, 0:NT * D].rearrange("p (t c) -> p t c", c=D)
        at1 = [0]

        def carve1(n):
            ap = big[:, at1[0]:at1[0] + n]
            at1[0] += n
            assert at1[0] <= ACCW
            return ap

        ed = [carve1(CH) for _ in range(2)]
        edT = [carve1(CH) for _ in range(2)]
        Xs = carve1(CH)
        Ex = [carve1(CH) for _ in range(2)]
        Y = carve1(CH)
        V = [carve1(SPC * P).rearrange("p (s c) -> p s c", c=P) for _ in range(2)]
        assert at1[0] <= ACCW
        x1T = big[:, 2 * CH:2 * CH + NG * PAIRS * P]
        at[0] = 4 * SPC * XW
        reach2 = carve(2 * NCH)[0:1, :].rearrange("p (h k) -> p h k", h=2)
        drow = carve(HT * 2 + 1, i32)
        negs = carve(HT * 2, bf16)
        rows_dst = carve(BLK * P, i32).rearrange("p (b j) -> p b j", j=P)
        rowf = carve(BLK * P).rearrange("p (b j) -> p b j", j=P)
        dT = carve(T)
        rows_src = hh[:, :, :].rearrange("p a b -> p (a b)")[:, NT * XW:NT * XW + BLK * P].bitcast(i32).rearrange(
            "p (b j) -> p b j", j=P)
        XG = 25
        xv = arena[:, 0:XG * D].rearrange("p (t c) -> p t c", c=D)
        xvd = big[:, NT * D:2 * NT * D].rearrange("p (t c) -> p t c", c=D)
        vsd = sb("vsd", [P, 2, D + 1])
        v_const = sb("v_const", [P, 2])
        node_sum = sb("node_sum", [P, 2, NT])
        sd_nodes = sb("sd_nodes", [P, NT])

        ps = ctx.enter_context(nc.psum_tensor("ps", [P, 8 * 512], f32))

        def bank(i, a=0, b=512):
            return ps[:, i * 512 + a:i * 512 + b]

        s_const = sem("const_ready")
        s_clear = sem("totals_cleared")
        s_w = sem("weights_loaded")
        s_watt = sem("attention_weights_loaded")
        s_vsp = sem("vsrc_product")
        s_xp = sem("x_by_partition_loaded")
        s_x = sem("x_loaded")
        s_drow = sem("dst_flat_loaded")
        s_pads = sem("pads_set")
        s_rsrc = sem("src_rows_loaded")
        s_rdst = sem("dst_rows_loaded")
        s_rtype = sem("type_rows_loaded")
        s_rowf = sem("rows_converted")
        s_rowT = sem("rows_transposed")
        s_srcT = sem("src_table")
        s_dT = sem("dst_transposed_out")
        s_tab = sem("tables_ready")
        s_xpart = sem("x_in_table")
        s_xones = sem("ones_in_table")
        s_vs = sem("attention_vectors_ready")
        s_negs = sem("flags_ready")
        s_negd = sem("flags_stored")
        s_cont = sem("cont_loaded")
        s_bc = sem("bases_broadcast")
        s_wT = sem("weights_transposed")
        s_wS = sem("weights_ready")
        s_xd = sem("x_times_vdst")
        s_sdn = sem("sdst_by_node")
        s_sdd = sem("sdst_stored")
        s_sdl = sem("sdst_everywhere")
        s_xpad = sem("x_padding_set")
        s_xtb = sem("xtab_built")
        s_xtd = sem("xtab_stored")
        s_dve = sem("dve_chain")
        layers = []
        for L in range(2):
            layers.append({n: sem(f"{n}{L}") for n in (
                "neg_loaded_0", "neg_loaded_1", "ix_ready", "rel_ready",
                "z_loaded_0", "z_loaded_1", "z_loaded_2", "z_loaded_3",
                "fwd_done", "max_done", "drop_ready", "bnd_done", "fac_product", "fac_ready",
                "onehot_ready", "sum_done", "acc_done",
                "merged_0", "merged", "n_product", "xn_ready", "sum_ready", "prodT", "prodTs", "w2_product", "x1_ready", "x1_kept",
                "x1T", "x1Ts", "h_product", "hl_product", "h_ready", "hl_ready", "h_stored", "rows_done",
                "dve_epi", "den_out", "share_ready", "mean_ready", "root_ready", "centred", "squared", "var_ready", "std_ready", "join_product", "join_done", "join_ready", "join_exp", "layer_done")})
        s_sdst_edge = sem("sdst_of_edges")
        s_score = sem("scores_ready")
        s_score_spread = sem("scores_spread")
        s_score_turned = sem("scores_turned")
        s_max_turned = sem("maxima_turned")
        s_exponent = sem("exponents_ready")
        s_exp = sem("exp_ready")
        s_score_part = sem("score_parts_done")
        s_edge_loaded = [sem("edge_loaded_0"), sem("edge_loaded_1")]
        s_edge_turned = sem("edges_turned")
        s_edge_out = sem("edges_turned_out")
        s_eh_turned = sem("eh_turned")
        s_eh_by_edge = sem("eh_by_edge")
        s_below_max = sem("below_maximum")
        s_exp_turned = sem("exp_turned")
        s_exp_by_edge = sem("exp_by_edge")
        s_exp_out = sem("exp_by_edge_out")
        s_sum_h_eh = sem("h_plus_eh")
        s_values = sem("values_ready")
        s_out = sem("out_stored")

        NCONST = 18

        s_apart = sem("apart")

        def apart(eng):
            eng.sem_inc(s_apart, 1)

        block = ctx.enter_context(nc.Block())

        def v3(t):
            return t.rearrange("p (t c) -> p t c", c=D)

        def spread(t):
            return t.unsqueeze(2).to_broadcast([P, GT, D])

        def chunk_meta(eng, k, count):
            _, got = nc.values_load_multi_w_load_instructions(
                meta[0:1, ds(k * META, count)], engines=[eng.engine], min_val=0, max_val=N,
                skip_runtime_bounds_check_because="dst values, N for padding, or a difference of two")
            return got

        def table(t, k):
            return t[:, ds(k * SPC, SPC)]

        @block.sync
        def _(sp):
            def tiles_of(rows_, arr, done):
                whole = E // P // P * P
                nb, rest = whole // P, E // P - whole
                sp.dma_start(rows_[:, 0:nb, :], arr[0:whole * P].rearrange("(b q j) -> q b j", q=P, j=P)).then_inc(done, 16)
                sp.dma_start(rows_[0:rest, nb, :],
                             arr[whole * P:(whole + rest) * P].rearrange("(q j) -> q j", j=P)).then_inc(done, 16)
                sp.dma_start(rows_[rest:rest + 1, nb, 0:E % P],
                             arr[(whole + rest) * P:E].rearrange("(q j) -> q j", q=1)).then_inc(done, 16)

            for view, w in ((wAtt[:, 0:D], Watt), (wa[:, 0:1], a[0:D, :]), (wa[:, 1:2], a[D:2 * D, :]),
                            (wAtt[:, D:D + 1], batt.rearrange("(o i) -> o i", i=1))):
                sp.dma_start(view, w).then_inc(s_watt, 16)
            sp.wait_ge(s_xpad, 1)
            full = N // NT
            for lo, hi in ((0, full // 16 * 16), (full // 16 * 16, full)):
                sp.dma_start(xp[lo:hi, :, :], x[lo * NT:hi * NT, :].rearrange("(p t) c -> p t c", t=NT)).then_inc(s_xp, 16)
            sp.dma_start(xp[full:full + 1, 0:N - full * NT, :],
                         x[full * NT:N, :].rearrange("(p t) c -> p t c", p=1)).then_inc(s_xp, 16)
            sp.wait_ge(s_const, 2)
            tiles_of(rows_src, src, s_rsrc)
            tiles_of(rows_dst, dst, s_rdst)
            sp.wait_ge(s_xones, 1)
            for i, lo in enumerate(range(0, NT, XG)):
                hi = min(lo + XG, NT)
                sp.wait_ge(s_xpart, 1 + i)
                sp.wait_ge(s_xtb, 1 + i)
                sp.dma_start(xtab.rearrange("(p t) c -> p t c", p=P)[:, lo:hi, :], xtb[:, lo:hi, :]).then_inc(s_xtd, 16)
            sp.wait_ge(s_const, 4)
            EP = T
            full = E // EP
            for lo, hi in ((0, full // 16 * 16), (full // 16 * 16, full)):
                sp.dma_start(drow[lo:hi, 1:EP + 1],
                             dst[lo * EP:hi * EP].rearrange("(p e) -> p e", e=EP)).then_inc(s_drow, 16)
            sp.dma_start(drow[full:full + 1, 1:E - full * EP + 1],
                         dst[full * EP:E].rearrange("(p e) -> p e", p=1)).then_inc(s_drow, 16)
            last = dst[0:(P - 1) * EP].rearrange("(p e) -> p e", e=EP)[:, EP - 1:EP]
            with nc.allow_non_contiguous_dma(reason="one element per partition"):
                sp.dma_start(drow[1:113, 0:1], last[0:112, :]).then_inc(s_drow, 16)
                sp.dma_start(drow[113:P, 0:1], last[112:P - 1, :]).then_inc(s_drow, 16)
            sp.wait_ge(s_pads, 1)
            tiles_of(rows_src, edge_type, s_rtype)
            sp.wait_ge(s_sdn, 1)
            sp.dma_start(sdd.rearrange("(p t) -> p t", p=P), sd_nodes[:, :]).then_inc(s_sdd, 16)
            sp.wait_ge(s_sdd, 16)
            sp.wait_ge(s_xpart, 2)
            sp.dma_start(sdst[:, 0:NPAD], sdd.rearrange("(o n) -> o n", o=1).to_broadcast([P, NPAD])).then_inc(s_sdl, 16)
            sp.wait_ge(s_negs, 1)
            sp.dma_start(negd.rearrange("(p e) -> p e", p=P), negs).then_inc(s_negd, 16)
            sp.wait_ge(s_negd, 16)
            sp.dma_start(cont[:, :], negd[HALF:HALF + 1].rearrange("(a b) -> a b", b=1).to_broadcast([P, 1])).then_inc(s_cont, 16)

            def load_flags(L, m, u):
                k, _, _, s2, n2 = lagged(m, u, 0)
                if live(m, k):
                    if late(m, n2):
                        sp.wait_ge(L["max_done"], k - 1)
                    for h in range(2):
                        part = negd[ds(h * HALF + k * CH, CH)].rearrange("(a e) -> a e", a=1)
                        sp.dma_start(neg[s2][h * D:(h + 1) * D, 0:CH], part.to_broadcast([D, CH])).then_inc(L[f"neg_loaded_{s2}"], 16)

            run_steps(sp, 0, lambda m, u: load_flags(layers[0], m, u))

            with sp.Fori(0, NG) as g:
                sp.wait_ge(layers[0]["h_ready"], g + 1)
                sp.dma_start(htab[ds(g * (GT * P), GT * P), :].rearrange("(t p) c -> p t c", p=P),
                             hs[:, ds(g * GT, GT), :]).then_inc(layers[0]["h_stored"], 16)

            def load_edges(m, u):
                load_flags(layers[1], m, u)
                k, _, _, s2, n2 = lagged(m, u, 0)
                if live(m, k):
                    if late(m, n2):
                        sp.wait_ge(s_edge_turned, k - 1)
                    by_half = ed[s2].rearrange("p (i h c) -> p i h c", i=TPC, h=2)
                    for h in range(2):
                        left = E - HALF - k * CH if h and isinstance(m, int) else CH
                        whole, rest = min(max(left, 0), CH) // P, min(max(left, 0), CH) % P
                        if whole:
                            sp.dma_start(by_half[:, 0:whole, h, :], edge_attr[ds(h * HALF + k * CH, whole * P), :].rearrange(
                                "(i p) c -> p i c", p=P)).then_inc(s_edge_loaded[s2], 16)
                        if rest:
                            sp.dma_start(by_half[0:rest, whole, h, :], edge_attr[E - rest:E, :]).then_inc(s_edge_loaded[s2], 16)

            sp.wait_ge(s_sdst_edge, NCH * SPC)
            run_steps(sp, 0, load_edges)

            for g in range(NG):
                sp.wait_ge(layers[1]["rows_done"], g + 1)
                full = min(GT, (N - g * GT * P) // P)
                sp.dma_start(out[g * GT * P:(g * GT + full) * P, :].rearrange("(t p) c -> p t c", p=P),
                             hs[:, g * GT:g * GT + full, :]).then_inc(s_out, 16)
            rest = N % P
            sp.dma_start(out[N - rest:N, :], hs[0:rest, NT - 1, :]).then_inc(s_out, 16)
            sp.wait_ge(s_out, 16 * (NG + 1))

        @block.gpsimd
        def _(g):
            g.memset(rows_src[:, BLK - 1, :], 0).then_inc(s_const, 1)
            g.memset(rows_dst[:, BLK - 1, :], N).then_inc(s_const, 1)
            g.memset(drow, N).then_inc(s_const, 1)
            g.wait_ge(s_const, 3)
            g.memset(drow[0:1, 0:1], -1).then_inc(s_const, 1)
            g.memset(ident[:, :], 0.0).then_inc(s_const, 1)
            g.wait_ge(s_const, 5)
            g.affine_select(out=ident[:, :], in_=ident[:, :], compare_op=ALU.not_equal, fill=1.0,
                            base=0, pattern=[[-1, P]], channel_multiplier=1).then_inc(s_const, 1)
            g.iota(iota_i[:, :], pattern=[[1, P]], base=0, channel_multiplier=0).then_inc(s_const, 1)
            for t, value in ((ones[:, :], 1.0), (tiny[:, :], 1e-30), (WRd[:, :], 0.0), (bndM[:, :], -BIG), (neg[0][:, CH:CH + 1], 0.0),
                             (neg[1][:, CH:CH + 1], 0.0), (W1b[:, :], 0.0), (xs[:, NT - 1, :], 0.0),
                             (W2d[:, :], 0.0), (WHd[:, :], 0.0), (WLd[:, :], 0.0)):
                g.memset(t, value).then_inc(s_const, 1)
            g.memset(xtb[:, :, D:D + 1], 1.0).then_inc(s_xones, 1)
            g.memset(acc[1][:, :], 0.0).then_inc(s_clear, 1)
            g.wait_ge(s_xp, 48)
            g.wait_ge(s_vs, 1)
            g.tensor_tensor(xvd, xp, vsd[:, 1:2, 0:D].to_broadcast([P, NT, D]), ALU.mult).then_inc(s_xd, 1)
            g.memset(acc[0][:, :], 0.0).then_inc(s_clear, 1)

            def gather(L, tab, zz, m, u):
                k, s4, n4, _, _ = lagged(m, u, 0)
                if not live(m, k):
                    return
                g.wait_ge(L["ix_ready"], k + 1)
                if late(m, n4):
                    g.wait_ge(L["sum_done"] if zz is z0 else s_sum_h_eh, k - 3)
                apart(g)
                for s in whole_slots(m, k):
                    w = XW if zz is z0 else D
                    g.indirect_dma_start(zz[s4][:, s, 0:w], None, tab[:, :],
                                         bass.IndirectOffsetOnAxis(ap=ixb[s4][:, s:s + 1], axis=0)
                                         ).then_inc(L[f"z_loaded_{s4}"], 16)

            g.wait_ge(s_xtd, 32)
            run_steps(g, 0, lambda m, u: gather(layers[0], xtab, z0, m, u))

            def merge(L, t, rows_):
                if t < NG:
                    if t >= 2:
                        g.wait_ge(L["n_product"], t - 1)
                    cols = slice(t * GT * P, (t + 1) * GT * P)
                    g.tensor_tensor(merged[t % 2][0:rows_, :], acc[0][0:rows_, cols], acc[1][0:rows_, cols], ALU.add).then_inc(L["merged"], 1)

            L = layers[0]
            g.wait_ge(L["join_done"], 1)
            merge(L, 1, D + 1)
            for t in range(NG):
                if t >= 2:
                    g.wait_ge(L["centred"], t - 1)
                g.tensor_tensor(v3(summed[t % 2]), xs[:, t * GT:(t + 1) * GT, :], b2b[:, :].unsqueeze(1).to_broadcast([P, GT, D]),
                                ALU.add).then_inc(L["sum_ready"], 1)
                g.wait_ge(L["sum_ready"], 2 * t + 1)
                g.wait_ge(L["xn_ready"], t + 1)
                g.tensor_tensor(summed[t % 2], summed[t % 2], share[t % 2], ALU.add).then_inc(L["sum_ready"], 1)
                merge(L, t + 2, D + 1)
            g.wait_ge(L["merged"], NG - 1)
            g.wait_ge(L["merged_0"], 1)
            g.memset(acc[1][:, :], 0.0).then_inc(L["rows_done"], 1)
            g.wait_ge(L["h_stored"], 16 * NG)
            run_steps(g, 0, lambda m, u: gather(layers[1], htab, z1, m, u))

            L = layers[1]
            g.wait_ge(L["join_done"], 1)
            merge(L, 1, P)
            for t in range(NG + 2):
                q, f = t - 1, t - 2
                if t < NG:
                    g.wait_ge(L["share_ready"], t + 1)
                    cell = v3(prod[t % 2])[:, 0:GT, :]
                    g.tensor_tensor(cell, cell, hl[:, t * GT:(t + 1) * GT, :], ALU.add).then_inc(L["sum_ready"], 1)
                if f >= 0:
                    g.wait_ge(L["root_ready"], f + 1)
                    g.tensor_tensor(hs[:, f * GT:(f + 1) * GT, :], v3(ybuf[f % 2]), spread(small[f % 2][:, 4 * GT:5 * GT]),
                                    ALU.mult).then_inc(L["rows_done"], 1)
                if 0 <= q < NG:
                    g.wait_ge(L["mean_ready"], q + 1)
                    y = v3(ybuf[q % 2])
                    g.tensor_tensor(y, y, spread(small[q % 2][:, GT:2 * GT]), ALU.subtract).then_inc(L["centred"], 1)
                merge(L, t + 2, P)

        @block.scalar
        def _(act):
            for view, w in ((wW1, W1), (wW2[:, 0:D], W2), (wW2[:, D:P], W2), (wWfc[:, 0:D], Wfc), (wWfc[:, D:P], Wfc),
                            (wWfcr[:, 0:D], Wfcr), (wWfcr[:, D:P], Wfcr), (loopS[:, :], loopW),
                            (b2b[:, :], b2.rearrange("(i o) -> i o", i=1).to_broadcast([P, D]))):
                act.dma_start(view, w).then_inc(s_w, 16)
            act.wait_ge(s_const, NCONST)
            act.dma_start(W1b[D:D + 1, 0:D], b1.rearrange("(i o) -> i o", i=1)).then_inc(s_w, 16)
            act.wait_ge(s_xp, 48)
            for lo in range(0, NT, XG):
                hi = min(lo + XG, NT)
                act.activation(xtb[:, lo:hi, 0:D], xp[:, lo:hi, :], ACT.Copy).then_inc(s_xpart, 1)
            act.wait_ge(s_srcT, 1)
            for k in range(4):
                act.activation(ixb[k][:, :], table(srcT, k), ACT.Copy).then_inc(layers[0]["ix_ready"], 1)
            full = (NT - 1) * P
            act.dma_start(xs[:, 0:NT - 1, :], x[0:full, :].rearrange("(t p) c -> p t c", p=P)).then_inc(s_x, 16)
            act.dma_start(xs[0:N - full, NT - 1, :], x[full:N, :]).then_inc(s_x, 16)

            def copy_params(L, m, u):
                k, s4, n4, _, _ = lagged(m, u, 0)
                if live(m, k):
                    if late(m, n4):
                        act.wait_ge(L[f"z_loaded_{s4}"], n4 * (16 * SPC))
                        act.wait_ge(L["onehot_ready"], (k - 3) * SPC)
                    if late(m, n4):
                        act.activation(ixb[s4][:, :], table(srcT, k), ACT.Copy).then_inc(L["ix_ready"], 1)
                    act.activation(relb[s4][:, :], table(relT, k), ACT.Copy).then_inc(L["rel_ready"], 1)
                    act.activation(relc[s4][:, :], table(relC, k), ACT.Copy).then_inc(L["rel_ready"], 1)

            def exp_fac(L, m, u, lag):
                k, _, _, s2, n2 = lagged(m, u, lag)
                if live(m, k):
                    act.wait_ge(L["fac_product"], k + 1)
                    if late(m, n2):
                        act.wait_ge(L["acc_done"], (k - 1) * SPC)
                    act.activation(fac[:, 2 * s2:2 * s2 + 2], bank(7, 0, 2), ACT.Exp,
                                   scale=-1.0).then_inc(L["fac_ready"], 1)

            def step0(m, u):
                L = layers[0]
                copy_params(L, m, u)
                k, _, _, s2, n2 = lagged(m, u, 3)
                if live(m, k):
                    act.wait_ge(s_exponent, k + 1)
                    if late(m, n2):
                        act.wait_ge(L["onehot_ready"], (k - 1) * SPC)
                    act.activation(pe_[:, s2 * SPC:(s2 + 1) * SPC], pd[:, s2 * SPC:(s2 + 1) * SPC], ACT.Exp).then_inc(s_exp, 1)
                exp_fac(L, m, u, 3)
                k, _, _, s2, _ = lagged(m, u, 2)
                if live(m, k):
                    act.wait_ge(s_score, k + 1)
                    if late(m, k):
                        act.wait_ge(s_score_turned, k)
                    act.activation(eb.rearrange("p (s c) -> p s c", c=D),
                                   es[:, s2 * SPC:(s2 + 1) * SPC].unsqueeze(2).to_broadcast([P, SPC, D]),
                                   ACT.Copy).then_inc(s_score_spread, 1)

            act.wait_ge(s_tab, 1)
            run_steps(act, 3, step0)

            def join_exp(L):
                act.wait_ge(L["join_ready"], 1)
                act.activation(join[:, 6:8], join[:, 4:6], ACT.Exp).then_inc(L["join_exp"], 1)

            def square_and_root(L, t):
                act.wait_ge(L["centred"], t + 1)
                if t >= 2:
                    act.wait_ge(L["var_ready"], t - 1)
                act.activation(square[t % 2], ybuf[t % 2], ACT.Square).then_inc(L["squared"], 1)
                act.wait_ge(L["var_ready"], t + 1)
                act.activation(small[t % 2][:, 4 * GT:5 * GT], small[t % 2][:, 3 * GT:4 * GT], ACT.Sqrt).then_inc(L["std_ready"], 1)

            L = layers[0]
            join_exp(L)
            for t in range(NG + 2):
                q, r = t - 1, t - 2
                if t < NG:
                    act.wait_ge(L["prodT"], t + 1)
                    if t:
                        act.wait_ge(L["w2_product"], t)
                    act.activation(prodT[:, :], bank(2, 0, PAIRS * P), ACT.Copy).then_inc(L["prodTs"], 1)
                if 0 <= q < NG:
                    square_and_root(L, q)
                if r >= 0:
                    act.wait_ge(L["h_product"], r + 1)
                    act.activation(hs[:, r * GT:(r + 1) * GT, :], v3(bank(6 + r % 2, 0, GT * D)), ACT.Copy).then_inc(L["h_ready"], 1)
                if 0 <= q < NG:
                    act.wait_ge(L["x1T"], q + 1)
                    act.activation(x1T[:, q * PAIRS * P:(q + 1) * PAIRS * P], bank(3, 0, PAIRS * P), ACT.Copy).then_inc(L["x1Ts"], 1)
                    act.activation(xs[:, q * GT:(q + 1) * GT, :], v3(x1b[q % 2])[:, 0:GT, :], ACT.Copy).then_inc(L["x1_kept"], 1)
            for k in range(4):
                act.activation(ixb[k][:, :], table(srcT, k), ACT.Copy).then_inc(layers[1]["ix_ready"], 1)
            for q in range(NG):
                act.wait_ge(L["hl_product"], q + 1)
                act.activation(hl[:, q * GT:(q + 1) * GT, :], v3(bank(6 + (NG + q) % 2, 0, GT * D)), ACT.Copy).then_inc(L["hl_ready"], 1)

            def step1(m, u):
                L = layers[1]
                copy_params(L, m, u)
                k, _, _, s2, n2 = lagged(m, u, 2)
                if live(m, k):
                    act.wait_ge(s_exp_by_edge, k + 1)
                    if late(m, n2):
                        act.wait_ge(L["sum_done"], k - 1)
                    act.activation(V[s2][:, :, D:P], bank(4).rearrange("p (s c) -> p s c", c=D), ACT.Copy).then_inc(s_exp_out, 1)
                exp_fac(L, m, u, 2)
                k, _, _, s2, n2 = lagged(m, u, 0)
                if live(m, k):
                    act.wait_ge(s_edge_turned, k + 1)
                    if late(m, n2):
                        act.wait_ge(s_eh_by_edge, k - 1)
                    act.activation(edT[s2], bank(0), ACT.Copy).then_inc(s_edge_out, 1)
                k, _, _, s2, n2 = lagged(m, u, 1)
                if live(m, k):
                    act.wait_ge(s_below_max, k + 1)
                    if late(m, n2):
                        act.wait_ge(s_exp_by_edge, k - 1)
                    act.activation(Ex[s2], Xs, ACT.Exp).then_inc(s_exp_turned, 1)

            run_steps(act, 3, step1)
            L = layers[1]
            join_exp(L)
            for t in range(NG + 2):
                if t < NG:
                    act.wait_ge(L["n_product"], t + 1)
                    if t >= 2:
                        act.wait_ge(L["share_ready"], t - 1)
                    nb = ps[:, t % 2 * 1024:t % 2 * 1024 + GT * P].rearrange("p (t c) -> p t c", c=P)
                    act.activation(v3(share[t % 2]), nb[:, :, D:P], ACT.Identity, bias=tiny[:, :]).then_inc(L["den_out"], 1)
                if t >= 2:
                    square_and_root(L, t - 2)

        @block.tensor
        def _(pe):
            pe.wait_ge(s_const, NCONST)

            def rows_transposed(n):
                pe.wait_ge(s_rowf, n)
                for b in range(BLK):
                    q = min(P, T - b * P)
                    last = pe.transpose(ps[:, b * P:b * P + q], rowf[0:q, b, :], ident[0:q, 0:q])
                last.then_inc(s_rowT, 1)

            pe.wait_ge(s_watt, 16 * 4)
            pe.matmul(bank(7, 0, D + 1), wa[:, 0:1].to_broadcast([D, P]), wAtt, start=True, stop=True)
            pe.matmul(bank(7, D + 1, 2 * D + 2), wa[:, 1:2].to_broadcast([D, P]), wAtt, start=True, stop=True).then_inc(s_vsp, 1)
            rows_transposed(1)
            pe.wait_ge(s_w, 16 * 10)
            pe.transpose(bank(6, 0, D)[0:D, :], wW1, ident[0:D, 0:D])
            for i, w in enumerate((wW2, wWfc, wWfcr)):
                pe.transpose(bank(6, (i + 1) * D, (i + 2) * D), w, ident[0:D, 0:D])
            pe.matmul(bank(6, 4 * D, 5 * D), wWfc, loopS[:, :], start=True, stop=True).then_inc(s_wT, 1)
            pe.wait_ge(s_srcT, 1)
            rows_transposed(2)
            pe.wait_ge(s_wS, 1)
            pe.wait_ge(s_dT, 1)
            for b in range(-(-T // 512)):
                w = min(512, T - b * 512)
                last = pe.matmul(bank(4 + b, 0, w), ones[0:1, :], dT[0:1, b * 512:b * 512 + w], start=True, stop=True)
            last.then_inc(s_bc, 1)
            rows_transposed(3)

            def fac_products(L, m, u, lag):
                k, _, _, s2, n2 = lagged(m, u, lag)
                if live(m, k):
                    pe.wait_ge(L["drop_ready"], k + 1)
                    if late(m, k):
                        pe.wait_ge(L["fac_ready"], k)
                    for h in range(2):
                        last = pe.matmul(bank(7, h, h + 1), pick[:, h, :], drop[:, s2:s2 + 1], start=True, stop=True)
                    last.then_inc(L["fac_product"], 1)

            def sums(L, m, u, lag, lhs, slots, rows_):
                k, s4, _, s2, _ = lagged(m, u, lag)
                if live(m, k):
                    pe.wait_ge(L["onehot_ready"], (k + 1) * SPC)
                    if late(m, k):
                        pe.wait_ge(L["acc_done"], k * SPC)
                    b = s4 if slots == 4 else s2
                    apart(pe)
                    reach, = chunk_meta(pe, k, 1)
                    with pe.If(reach < NW):
                        for s in range(SPC):
                            last = pe.matmul(bank(5 + s % 2, 0, NW)[0:rows_, :], lhs[b][:, s, 0:rows_],
                                             oh[s2][:, s, 0:NW], start=s < 2, stop=s >= SPC - 2)
                        last.then_inc(L["sum_done"], 1)
                    with pe.Else():
                        for s in range(SPC):
                            last = pe.matmul(bank(5 + s % 2, s // 2 * P, (s // 2 + 1) * P)[0:rows_, :], lhs[b][:, s, 0:rows_],
                                             oh[s2][:, s, :], start=True, stop=True)
                        last.then_inc(L["sum_done"], 1)

            def step0(m, u):
                L = layers[0]
                k, _, _, s2, _ = lagged(m, u, 2)
                if live(m, k):
                    pe.wait_ge(s_score_spread, k + 1)
                    if late(m, k):
                        pe.wait_ge(L["fwd_done"], k)
                    for i in range(TPC):
                        last = pe.matmul(bank(0, i * P, (i + 1) * P), eb[:, i * P:(i + 1) * P], ident[:, :], start=True, stop=True)
                    last.then_inc(s_score_turned, 1)
                sums(L, m, u, 3, z0, 4, D + 1)
                k, _, _, s2, _ = lagged(m, u, 2)
                if live(m, k):
                    pe.wait_ge(L["max_done"], k + 1)
                    if late(m, k - 1):
                        pe.wait_ge(s_exponent, k - 1)
                    for i in range(TPC):
                        last = pe.matmul(bank(2 + s2, 2 * i, 2 * i + 2), M[s2][:, i * P:(i + 1) * P],
                                         ident[:, 0:P:D], start=True, stop=True)
                    last.then_inc(s_max_turned, 1)
                fac_products(L, m, u, 2)

            pe.wait_ge(s_tab, 1)
            run_steps(pe, 3, step0)

            def join_products(L):
                pe.wait_ge(L["bnd_done"], NCH)
                pe.wait_ge(L["fac_ready"], NCH)
                pe.matmul(bank(7, 100, 101), pick[:, 0, :], F[(NCH - 1) % 2][:, CH - 1:CH], start=True, stop=True)
                pe.matmul(bank(7, 101, 102), pick[:, 1, :], bndM[:, (NCH - 1) % 2:(NCH - 1) % 2 + 1], start=True, stop=True).then_inc(L["join_product"], 1)

            L = layers[0]
            join_products(L)

            def wait_merged(L, t):
                if t:
                    pe.wait_ge(L["merged"], t)
                else:
                    pe.wait_ge(L["merged_0"], 1)

            def n_products(t):
                wait_merged(L, t)
                if t >= 2:
                    pe.wait_ge(L["xn_ready"], t - 1)
                for i in range(GT):
                    last = pe.matmul(bank(t % 2, i * (D + 1), (i + 1) * (D + 1)), merged[t % 2][0:D + 1, i * P:(i + 1) * P], W1b[:, :],
                                     start=True, stop=True)
                last.then_inc(L["n_product"], 1)

            def x1_products(q, use, weights, done):
                for i in range(PAIRS):
                    last = pe.matmul(bank(6 + use % 2, i * P, (i + 1) * P), x1T[:, (q * PAIRS + i) * P:(q * PAIRS + i + 1) * P],
                                     weights[:, :], start=True, stop=True)
                last.then_inc(L[done], 1)

            n_products(0)
            n_products(1)
            for t in range(NG + 2):
                q, r = t - 1, t - 2
                if t < NG:
                    pe.wait_ge(L["xn_ready"], t + 1)
                    if t:
                        pe.wait_ge(L["prodTs"], t)
                    for i in range(PAIRS):
                        last = pe.transpose(bank(2, i * P, (i + 1) * P), prod[t % 2][:, i * P:(i + 1) * P], ident[:, :])
                    last.then_inc(L["prodT"], 1)
                if r >= 0:
                    pe.wait_ge(L["x1Ts"], r + 1)
                    if r >= 2:
                        pe.wait_ge(L["h_ready"], r - 1)
                    x1_products(r, r, WHd, "h_product")
                if t < NG:
                    pe.wait_ge(L["prodTs"], t + 1)
                    if t >= 2:
                        pe.wait_ge(L["centred"], t - 1)
                    for i in range(PAIRS):
                        last = pe.matmul(bank(4 + t % 2, i * P, (i + 1) * P), prodT[:, i * P:(i + 1) * P], W2d[:, :], start=True, stop=True)
                    last.then_inc(L["w2_product"], 1)
                if 0 <= q < NG:
                    pe.wait_ge(L["x1_ready"], q + 1)
                    if q:
                        pe.wait_ge(L["x1Ts"], q)
                    for i in range(PAIRS):
                        last = pe.transpose(bank(3, i * P, (i + 1) * P), x1b[q % 2][:, i * P:(i + 1) * P], ident[:, :])
                    last.then_inc(L["x1T"], 1)
                if t + 2 < NG:
                    n_products(t + 2)
            for q in range(NG):
                if q < 2:
                    pe.wait_ge(L["h_ready"], NG + q - 1)
                else:
                    pe.wait_ge(L["hl_ready"], q - 1)
                x1_products(q, NG + q, WLd, "hl_product")

            def step1(m, u):
                L = layers[1]
                k, _, _, s2, n2 = lagged(m, u, 1)
                if live(m, k):
                    pe.wait_ge(s_edge_out, k + 1)
                    if late(m, k):
                        pe.wait_ge(s_below_max, k)
                    pe.matmul(bank(1), WRd[:, :], edT[s2], start=True, stop=True).then_inc(s_eh_turned, 1)
                k, _, _, s2, _ = lagged(m, u, 2)
                if live(m, k):
                    pe.wait_ge(s_exp_turned, k + 1)
                    if late(m, k):
                        pe.wait_ge(s_exp_out, k)
                    for i in range(TPC):
                        last = pe.transpose(bank(4, i * P, (i + 1) * P), Ex[s2][:, i * P:(i + 1) * P], ident[:, :])
                    last.then_inc(s_exp_by_edge, 1)
                fac_products(L, m, u, 2)
                k, _, _, s2, n2 = lagged(m, u, 0)
                if live(m, k):
                    pe.wait_ge(s_edge_loaded[s2], n2 * 32 + 16 * edge_loads(m, k))
                    if late(m, k):
                        pe.wait_ge(s_edge_out, k)
                    for i in range(TPC):
                        last = pe.transpose(bank(0, i * P, (i + 1) * P), ed[s2][:, i * P:(i + 1) * P], ident[:, :])
                    last.then_inc(s_edge_turned, 1)
                k, _, _, s2, n2 = lagged(m, u, 1)
                if live(m, k):
                    if late(m, n2):
                        pe.wait_ge(s_sum_h_eh, k - 1)
                    for i in range(TPC):
                        last = pe.matmul(bank(2 + s2, i * P, (i + 1) * P), edT[s2][:, i * P:(i + 1) * P], WRd[:, :], start=True, stop=True)
                    last.then_inc(s_eh_by_edge, 1)
                k, _, _, s2, n2 = lagged(m, u, 3)
                if live(m, k):
                    pe.wait_ge(s_values, k + 1)
                sums(L, m, u, 3, V, 2, P)

            pe.wait_ge(layers[0]["layer_done"], 1)
            run_steps(pe, 3, step1)
            L = layers[1]
            join_products(L)
            for t in range(NG):
                wait_merged(L, t)
                if t >= 2:
                    pe.wait_ge(L["share_ready"], t - 1)
                for i in range(GT):
                    last = pe.transpose(ps[:, t % 2 * 1024 + i * P:t % 2 * 1024 + (i + 1) * P], merged[t % 2][:, i * P:(i + 1) * P], ident[:, :])
                last.then_inc(L["n_product"], 1)

        @block.vector
        def _(dve):
            chain = Chain(dve, s_dve)
            dve.memset(xp[96:P, N % NT:NT, :], 0.0).then_inc(s_xpad, 1)
            dve.memset(sdst[:, NPAD:ACCW], 0.0)
            dve.wait_ge(s_vsp, 1)
            chain(dve.tensor_copy(vsd[:, :, :], bank(7, 0, 2 * D + 2).rearrange("p (v c) -> p v c", v=2)))
            chain(dve.tensor_scalar(v_const[:, :], vsd[:, :, D], 0.125, None, ALU.mult))
            dve.sem_inc(s_vs, 1)
            dve.wait_ge(s_xp, 48)
            for t in range(0, NT, XG):
                n = min(XG, NT - t)
                chain(dve.tensor_tensor(xv[:, 0:n, :], xp[:, t:t + n, :], vsd[:, 0:1, 0:D].to_broadcast([P, n, D]), ALU.mult))
                chain(dve.tensor_reduce(node_sum[:, 0, t:t + n], xv[:, 0:n, :], AX.X, ALU.add))
                dve.tensor_scalar(xtb[:, t:t + n, D + 1], node_sum[:, 0, t:t + n], 0.125, v_const[:, 0:1],
                                  ALU.mult, ALU.add).then_inc(s_xtb, 1)
            dve.wait_ge(s_const, NCONST)
            dve.tensor_copy(iota[:, :], iota_i[:, :])
            for h in range(2):
                dve.tensor_copy(pick[:, h, :].rearrange("p (a c) -> p a c", a=2),
                                ident[:, h * D:(h + 1) * D].unsqueeze(1).to_broadcast([P, 2, D]))

            metas = meta[:, :].rearrange("p (k n) -> p k n", n=META)

            def halves(t):
                return [t.rearrange("p (t h) -> p h t", h=2)[:, h, :] for h in range(2)]

            dve.wait_ge(s_rsrc, 48)
            chain(dve.tensor_copy(rowf, rows_src))
            dve.sem_inc(s_rowf, 1)
            dve.memset(rows_src[:, BLK - 1, :], 1).then_inc(s_pads, 1)
            dve.wait_ge(s_xd, 1)
            chain(dve.tensor_reduce(node_sum[:, 1, :], xvd, AX.X, ALU.add))
            dve.tensor_scalar(sd_nodes[:, :], node_sum[:, 1, :], 0.125, v_const[:, 1:2], ALU.mult, ALU.add).then_inc(s_sdn, 1)
            dve.wait_ge(s_rowT, 1)
            for h in range(2):
                last = dve.tensor_copy(halves(srcT)[h], ps[:, h * HT:(h + 1) * HT])
            chain(last)
            dve.sem_inc(s_srcT, 1)
            dve.wait_ge(s_wT, 1)
            dve.tensor_copy(W1b[0:D, 0:D], bank(6, 0, D)[0:D, :])
            dve.memset(W1b[D:D + 1, D:D + 1], 1.0)
            for i, diagonal in enumerate((W2d, WHd, WRd, WLd)):
                for h in range(2):
                    last = dve.tensor_copy(diagonal[h * D:(h + 1) * D, h * D:(h + 1) * D],
                                           bank(6, (i + 1) * D, (i + 2) * D)[h * D:(h + 1) * D, :])
            chain(last)
            dve.sem_inc(s_wS, 1)
            dve.wait_ge(s_rdst, 48)
            chain(dve.tensor_copy(rowf, rows_dst))
            dve.sem_inc(s_rowf, 1)
            dve.wait_ge(s_rowT, 2)
            chain(dve.tensor_copy(dT, ps[:, 0:T]))
            dve.sem_inc(s_dT, 1)
            dve.wait_ge(s_rtype, 48)
            chain(dve.tensor_copy(rowf, rows_src))
            dve.sem_inc(s_rowf, 1)
            dve.wait_ge(s_drow, 16 * 5)
            differs = relC[:, :]
            chain(dve.tensor_tensor(differs, drow[:, 1:T + 1], drow[:, 0:T], ALU.not_equal))
            chain(dve.tensor_scalar(negs, differs, -BIG, None, ALU.mult))
            dve.sem_inc(s_negs, 1)
            dve.wait_ge(s_bc, 1)
            for h in range(2):
                base = ps[:, 4 * 512 + h * HT:4 * 512 + (h + 1) * HT]
                dve.tensor_tensor(halves(relT)[h], dT[:, h * HT:(h + 1) * HT], base, ALU.subtract)
                chain(dve.tensor_tensor(halves(relC)[h].rearrange("p (k i) -> p k i", i=TPC),
                                        dT[:, h * HT:(h + 1) * HT].rearrange("p (k i) -> p k i", i=TPC),
                                        base[:, ::TPC].unsqueeze(2).to_broadcast([P, NCH, TPC]), ALU.subtract))
                if h == 1:
                    chain(dve.tensor_copy(join[:, 0:1], base[:, 0:1]))
                    chain(dve.tensor_scalar(bnd[:, :], base[:, ::TPC], join[:, 0:1], -BIG, ALU.not_equal, ALU.mult))
                row = dT[0:1, h * HT:(h + 1) * HT].rearrange("p (k i) -> p k i", i=TPC)
                dve.tensor_copy(metas[:, :, 1:1 + SPC].rearrange("p k (i h) -> p h k i", h=2)[:, h, :, :], row)
                nxt = dT[0:1, (h + 1) * HT - (NCH - 1) * TPC:(h + 1) * HT:TPC] if h else dT[0:1, TPC:HT + 1:TPC]
                n_next = NCH - h
                dve.tensor_tensor(reach2[:, h, 0:n_next], nxt, dT[0:1, h * HT:h * HT + (n_next - 1) * TPC + 1:TPC], ALU.subtract)
            chain(dve.tensor_scalar(reach2[:, 1, NCH - 1:NCH], dT[0:1, T - TPC:T - TPC + 1], -1.0, float(N), ALU.mult, ALU.add))
            chain(dve.tensor_tensor(metas[:, :, 0], reach2[:, 0, :], reach2[:, 1, :], ALU.max))
            dve.wait_ge(s_rowT, 3)
            for h in range(2):
                last = dve.tensor_scalar(halves(biasT)[h], ps[:, h * HT:(h + 1) * HT], 0.0, 0.625, ALU.is_equal, ALU.mult)
            chain(last)
            dve.wait_ge(s_sdl, 16)
            dve.wait_ge(s_clear, 2)
            dve.wait_ge(s_negd, 16)
            dve.sem_inc(s_tab, 1)
            dve.wait_ge(s_cont, 16)

            def scans(L, m, u, lag, scores):
                k, _, _, s2, n2 = lagged(m, u, lag)
                dve.wait_ge(L[f"neg_loaded_{s2}"], (n2 + 1) * 32)
                first = -BIG if isinstance(k, int) and k == 0 else F[1 - s2][:, CH - 1:CH]
                if late(m, k - 1):
                    dve.wait_ge(L["bnd_done"], k)
                dve.tensor_tensor_scan(F[s2], neg[s2][:, 0:CH], scores, first, ALU.add, ALU.max).then_inc(L["fwd_done"], 1)
                dve.wait_ge(L["fwd_done"], k + 1)
                dve.tensor_tensor_scan(M[s2][:, ::-1], neg[s2][:, CH:0:-1], F[s2][:, ::-1], F[s2][:, CH - 1:CH],
                                       ALU.add, ALU.max).then_inc(L["max_done"], 1)
                dve.wait_ge(L["max_done"], k + 1)
                prev = -BIG if isinstance(k, int) and k == 0 else F[1 - s2][:, CH - 1:CH]
                if late(m, n2):
                    dve.wait_ge(L["fac_product"], k - 1)
                if isinstance(k, int) and k == 0:
                    dve.memset(drop[:, 0:1], 0.0).then_inc(L["drop_ready"], 1)
                else:
                    dve.tensor_scalar(drop[:, s2:s2 + 1], M[s2][:, 0:1], prev, 0.0, ALU.subtract, ALU.max).then_inc(L["drop_ready"], 1)
                dve.scalar_tensor_tensor(bndM[:, s2:s2 + 1], M[s2][:, 0:1], bnd[:, ds(k, 1)], bndM[:, 1 - s2:2 - s2],
                                         ALU.add, ALU.max).then_inc(L["bnd_done"], 1)

            def add_windows(L, m, u, lag, rows_):
                k, _, _, s2, _ = lagged(m, u, lag)
                if not live(m, k):
                    return
                dve.wait_ge(L["sum_done"], k + 1)
                dve.wait_ge(L["fac_ready"], k + 1)
                apart(dve)
                reach, *at_ = chunk_meta(dve, k, 1 + SPC)
                with dve.If(reach < NW):
                    if late(m, k):
                        dve.wait_ge(L["acc_done"], k * SPC)
                    for h in range(2):
                        win = acc[h][0:rows_, ds(at_[h], NW)]
                        dve.scalar_tensor_tensor(win, win, fac[0:rows_, 2 * s2 + h:2 * s2 + h + 1], bank(5 + h, 0, NW)[0:rows_, :],
                                                 ALU.mult, ALU.add).then_inc(L["acc_done"], TPC)
                with dve.Else():
                    for s in range(SPC):
                        h = s % 2
                        win = acc[h][0:rows_, ds(at_[s], P)]
                        new = bank(5 + h, s // 2 * P, (s // 2 + 1) * P)[0:rows_, :]
                        if not (isinstance(k, int) and k == 0 and s < 2):
                            dve.wait_ge(L["acc_done"], k * SPC + s - 1)
                        if s < 2:
                            dve.scalar_tensor_tensor(win, win, fac[0:rows_, 2 * s2 + h:2 * s2 + h + 1], new,
                                                     ALU.mult, ALU.add).then_inc(L["acc_done"], 1)
                        else:
                            dve.tensor_tensor(win, win, new, ALU.add).then_inc(L["acc_done"], 1)

            def step0(m, u):
                L = layers[0]
                k, _, _, s2, n2 = lagged(m, u, 3)
                sl = slice(s2 * SPC, (s2 + 1) * SPC)
                if live(m, k):
                    dve.wait_ge(s_max_turned, k + 1)
                    if late(m, n2):
                        dve.wait_ge(s_exp, k - 1)
                    dve.tensor_tensor(pd[:, sl], es[:, sl], bank(2 + s2, 0, SPC), ALU.subtract).then_inc(s_exponent, 1)
                k, s4, n4, s2, n2 = lagged(m, u, 2)
                sl = slice(s2 * SPC, (s2 + 1) * SPC)
                if live(m, k):
                    dve.wait_ge(L[f"z_loaded_{s4}"], n4 * (16 * SPC) + 16 * len(whole_slots(m, k)))
                    dve.wait_ge(s_sdst_edge, (k + 1) * SPC)
                    dve.tensor_tensor(ts[:, sl], us[:, sl], z0[s4][:, :, D + 1], ALU.add).then_inc(s_score_part, 1)
                    dve.wait_ge(s_score_part, 2 * k + 1)
                    dve.tensor_tensor(ubb[:, sl], ts[:, sl], table(biasT, k), ALU.add).then_inc(s_score_part, 1)
                    dve.wait_ge(s_score_part, 2 * k + 2)
                    if late(m, n2):
                        dve.wait_ge(s_exponent, k - 1)
                    dve.scalar_tensor_tensor(es[:, sl], ubb[:, sl], 0.2, ubb[:, sl], ALU.mult, ALU.max).then_inc(s_score, 1)
                k, s4, _, s2, n2 = lagged(m, u, 3)
                if live(m, k):
                    dve.wait_ge(s_exp, k + 1)
                    if late(m, n2):
                        dve.wait_ge(L["sum_done"], k - 1)
                    apart(dve)
                    reach, = chunk_meta(dve, k, 1)
                    with dve.If(reach < NW):
                        dve.tensor_tensor(oh[s2][:, :, 0:NW], ohn[s4], pe_[:, s2 * SPC:(s2 + 1) * SPC].unsqueeze(2).to_broadcast([P, SPC, NW]),
                                          ALU.mult).then_inc(L["onehot_ready"], SPC)
                    with dve.Else():
                        for s in range(SPC):
                            dve.tensor_scalar(oh[s2][:, s, :], iota[:, :], relb[s4][:, s:s + 1],
                                              pe_[:, s2 * SPC + s:s2 * SPC + s + 1], ALU.is_equal, ALU.mult).then_inc(L["onehot_ready"], 1)
                k, s4, _, s2, _ = lagged(m, u, 1)
                if live(m, k):
                    dve.wait_ge(L["rel_ready"], 2 * k + 2)
                    apart(dve)
                    reach, *at_ = chunk_meta(dve, k, 1 + SPC)
                    mine = us[:, s2 * SPC:(s2 + 1) * SPC]
                    with dve.If(reach < NW):
                        dve.tensor_tensor(ohn[s4], iota[:, 0:NW].unsqueeze(1).to_broadcast([P, SPC, NW]),
                                          relc[s4][:, :].unsqueeze(2).to_broadcast([P, SPC, NW]), ALU.is_equal).then_inc(s_sdst_edge, 1)
                        dve.wait_ge(s_sdst_edge, k * SPC + 1)
                        both = junk.rearrange("p (i h w) -> p h i w", h=2, w=NW)
                        for h in range(2):
                            dve.tensor_tensor(both[:, h, :, :], ohn[s4].rearrange("p (i h) w -> p h i w", h=2)[:, h, :, :],
                                              sdst[:, ds(at_[h], NW)].unsqueeze(1).to_broadcast([P, TPC, NW]), ALU.mult).then_inc(s_sdst_edge, 1)
                        dve.wait_ge(s_sdst_edge, k * SPC + 3)
                        dve.tensor_reduce(mine, junk.rearrange("p (s w) -> p s w", w=NW), AX.X, ALU.add).then_inc(s_sdst_edge, SPC - 3)
                    with dve.Else():
                        for s in range(SPC):
                            if not (isinstance(k, int) and k == 0 and s < 2):
                                dve.wait_ge(s_sdst_edge, k * SPC + s - 1)
                            dve.scalar_tensor_tensor(junk[:, s % 2 * P:(s % 2 + 1) * P], iota[:, :], relb[s4][:, s:s + 1],
                                                     sdst[:, ds(at_[s], P)], ALU.is_equal, ALU.mult,
                                                     accum_out=mine[:, s:s + 1]).then_inc(s_sdst_edge, 1)
                k, _, _, s2, _ = lagged(m, u, 2)
                if live(m, k):
                    dve.wait_ge(s_score_turned, k + 1)
                    if late(m, k - 1):
                        dve.wait_ge(s_max_turned, k - 1)
                    scans(L, m, u, 2, bank(0))
                add_windows(L, m, u, 3, D + 1)

            run_steps(dve, 3, step0)

            def join_halves(L, rows_, chain):
                dve.wait_ge(L["join_product"], 1)
                dve.wait_ge(L["acc_done"], NCH * SPC)
                chain(dve.tensor_copy(join[:, 0:2], bank(7, 100, 102)))
                chain(dve.tensor_tensor(join[:, 2:3], join[:, 0:1], cont[:, 0:1], ALU.add))
                chain(dve.tensor_tensor(join[:, 3:4], join[:, 2:3], join[:, 1:2], ALU.max))
                chain(dve.tensor_tensor(join[:, 4:5], join[:, 2:3], join[:, 3:4], ALU.subtract))
                chain(dve.tensor_tensor(join[:, 5:6], join[:, 1:2], join[:, 3:4], ALU.subtract))
                dve.sem_inc(L["join_ready"], 1)
                dve.wait_ge(L["join_exp"], 1)
                apart(dve)
                at_ = chunk_meta(dve, 0, 3)[2:]
                for h in range(2):
                    one = acc[h][0:rows_, ds(at_[0], 1)]
                    chain(dve.tensor_scalar(one, one, join[0:rows_, 6 + h:7 + h], None, ALU.mult))
                dve.sem_inc(L["join_done"], 1)
                dve.tensor_tensor(merged[0][0:rows_, :], acc[0][0:rows_, 0:GT * P], acc[1][0:rows_, 0:GT * P],
                                  ALU.add).then_inc(L["merged_0"], 1)

            def mean(L, chain, t):
                sm = small[t % 2][:, GT:2 * GT]
                chain(dve.tensor_reduce(sm, v3(ybuf[t % 2]), AX.X, ALU.add))
                return dve.tensor_scalar(sm, sm, 1.0 / D, None, ALU.mult)

            def centre(L, chain, t):
                chain(mean(L, chain, t))
                y = v3(ybuf[t % 2])
                dve.tensor_tensor(y, y, spread(small[t % 2][:, GT:2 * GT]), ALU.subtract).then_inc(L["centred"], 1)

            def variance(L, chain, t):
                sm = small[t % 2]
                dve.wait_ge(L["squared"], t + 1)
                chain(dve.tensor_reduce(sm[:, 2 * GT:3 * GT], v3(square[t % 2]), AX.X, ALU.add))
                dve.tensor_scalar(sm[:, 3 * GT:4 * GT], sm[:, 2 * GT:3 * GT], 1.0 / D, 1e-5, ALU.mult, ALU.add).then_inc(L["var_ready"], 1)

            def reciprocal_root(L, t):
                root = small[t % 2][:, 4 * GT:5 * GT]
                dve.wait_ge(L["std_ready"], t + 1)
                return dve.reciprocal(root, root)

            def scale(L, chain, t, dest):
                chain(reciprocal_root(L, t))
                return dve.tensor_tensor(dest, v3(ybuf[t % 2]), spread(small[t % 2][:, 4 * GT:5 * GT]), ALU.mult)

            dve.wait_ge(s_x, 32)
            L = layers[0]
            chain = Chain(dve, L["dve_epi"])
            join_halves(L, D + 1, chain)
            for b in prod + x1b:
                last = dve.memset(b[:, GT * D:PAIRS * P], 0.0)
            chain(last)

            def neighbours(t):
                dve.wait_ge(L["n_product"], t + 1)
                nb = bank(t % 2, 0, GT * (D + 1)).rearrange("p (t c) -> p t c", c=D + 1)
                rden = small[t % 2][:, 0:GT]
                dve.tensor_scalar(no_edge[:, t * GT:(t + 1) * GT], nb[:, :, D], 0.0, None, ALU.is_equal)
                chain(dve.tensor_scalar(rden, nb[:, :, D], 1e-9, None, ALU.add))
                chain(dve.reciprocal(rden, rden))
                if t >= 2:
                    dve.wait_ge(L["sum_ready"], 2 * (t - 1))
                chain(dve.tensor_tensor(v3(share[t % 2]), nb[:, :, 0:D], spread(rden), ALU.mult))
                if t >= 2:
                    dve.wait_ge(L["prodT"], t - 1)
                dve.tensor_tensor(v3(prod[t % 2])[:, 0:GT, :], v3(share[t % 2]), xs[:, t * GT:(t + 1) * GT, :],
                                  ALU.mult).then_inc(L["xn_ready"], 1)

            neighbours(0)
            neighbours(1)
            for q in range(NG):
                y = ybuf[q % 2]
                dve.wait_ge(L["w2_product"], q + 1)
                dve.wait_ge(L["sum_ready"], 2 * (q + 1))
                chain(dve.tensor_tensor(y, summed[q % 2], bank(4 + q % 2, 0, GT * D), ALU.add))
                chain(dve.scalar_tensor_tensor(y, y, 0.2, y, ALU.mult, ALU.max))
                chain(dve.tensor_tensor(v3(y), v3(y), xs[:, q * GT:(q + 1) * GT, :], ALU.add))
                centre(L, chain, q)
                if q + 2 < NG:
                    neighbours(q + 2)
                if q >= 2:
                    dve.wait_ge(L["x1_kept"], q - 1)
                variance(L, chain, q)
                scale(L, chain, q, v3(x1b[q % 2])[:, 0:GT, :]).then_inc(L["x1_ready"], 1)
            dve.wait_ge(L["merged"], NG - 1)
            dve.memset(acc[0][:, :], 0.0)
            chain(dve.memset(bndM[:, :], -BIG))
            for t in range(NG):
                dve.wait_ge(L["hl_ready"], t + 1)
                apart(dve)
                dve.copy_predicated(hl[:, t * GT:(t + 1) * GT, :], spread(no_edge[:, t * GT:(t + 1) * GT].bitcast(u32)),
                                    hs[:, t * GT:(t + 1) * GT, :])
            dve.wait_ge(L["rows_done"], 1)
            dve.sem_inc(L["layer_done"], 1)

            def step1(m, u):
                L = layers[1]
                k, _, _, s2, _ = lagged(m, u, 1)
                if live(m, k):
                    dve.wait_ge(s_eh_turned, k + 1)
                    scans(L, m, u, 1, bank(1))
                    if late(m, k):
                        dve.wait_ge(s_exp_turned, k)
                    dve.tensor_tensor(Xs, bank(1), M[s2], ALU.subtract).then_inc(s_below_max, 1)
                k, s4, n4, s2, n2 = lagged(m, u, 2)
                if live(m, k):
                    dve.wait_ge(L[f"z_loaded_{s4}"], n4 * (16 * SPC) + 16 * len(whole_slots(m, k)))
                    dve.wait_ge(s_eh_by_edge, k + 1)
                    if late(m, k):
                        dve.wait_ge(s_values, k)
                    dve.tensor_tensor(Y, bank(2 + s2), z[s4][:, 0:SPC * D], ALU.add).then_inc(s_sum_h_eh, 1)
                    dve.wait_ge(L["rel_ready"], 2 * k + 2)
                    if late(m, n2):
                        dve.wait_ge(L["sum_done"], k - 1)
                    apart(dve)
                    reach, = chunk_meta(dve, k, 1)
                    with dve.If(reach < NW):
                        dve.tensor_tensor(oh[s2][:, :, 0:NW], iota[:, 0:NW].unsqueeze(1).to_broadcast([P, SPC, NW]),
                                          relc[s4][:, :].unsqueeze(2).to_broadcast([P, SPC, NW]), ALU.is_equal
                                          ).then_inc(L["onehot_ready"], SPC)
                    with dve.Else():
                        for s in range(SPC):
                            dve.tensor_scalar(oh[s2][:, s, :], iota[:, :], relb[s4][:, s:s + 1], None,
                                              ALU.is_equal).then_inc(L["onehot_ready"], 1)
                    dve.wait_ge(s_exp_out, k + 1)
                    dve.wait_ge(s_sum_h_eh, k + 1)
                    dve.tensor_tensor(V[s2][:, :, 0:D], V[s2][:, :, D:P], Y.rearrange("p (s c) -> p s c", c=D),
                                      ALU.mult).then_inc(s_values, 1)
                add_windows(L, m, u, 3, P)

            run_steps(dve, 3, step1)

            L = layers[1]
            chain = Chain(dve, L["dve_epi"])
            join_halves(L, P, chain)
            for t in range(NG + 2):
                q, f = t - 1, t - 2
                if t < NG:
                    dve.wait_ge(L["den_out"], t + 1)
                    nb = ps[:, t % 2 * 1024:t % 2 * 1024 + GT * P].rearrange("p (t c) -> p t c", c=P)
                    cell = v3(share[t % 2])
                    chain(dve.reciprocal(cell, cell))
                if f >= 0:
                    variance(L, chain, f)
                if t < NG:
                    dve.tensor_tensor(v3(prod[t % 2])[:, 0:GT, :], nb[:, :, 0:D], cell, ALU.mult).then_inc(L["share_ready"], 1)
                if f >= 0:
                    reciprocal_root(L, f).then_inc(L["root_ready"], 1)
                if 0 <= q < NG:
                    dve.wait_ge(L["sum_ready"], q + 1)
                    if q >= 2:
                        dve.wait_ge(L["rows_done"], q - 1)
                    y = v3(ybuf[q % 2])
                    chain(dve.scalar_tensor_tensor(y, v3(prod[q % 2])[:, 0:GT, :], 0.0, xs[:, q * GT:(q + 1) * GT, :], ALU.max, ALU.add))
                    mean(L, chain, q).then_inc(L["mean_ready"], 1)


_INS = ['x', 'src', 'dst', 'edge_attr_64', 'edge_type_4', 'L0_gnn_W1_w', 'L0_gnn_W1_b', 'L0_gnn_W2_w', 'L0_gnn_W2_b',
        'L0_gnn_W_att_w', 'L0_gnn_W_att_b', 'L0_gnn_a', 'L1_gnn_W_fc', 'L1_gnn_W_fcr', 'L1_gnn_loop_W']
_OUTS = [((N, D), 'float32')]


def kernel(**inputs):
    import numpy as _np
    import concourse.bacc as _bacc
    from concourse import mybir as _mybir
    from concourse.bass_utils import run_bass_kernel_spmd as _run

    nc = _bacc.Bacc("TRN2", target_bir_lowering=False, num_devices=1)
    arrays, args = {}, []
    for name in _INS:
        a = _np.ascontiguousarray(inputs[name])
        arrays[f"in_{name}_dram"] = a
        args.append(nc.dram_tensor(f"in_{name}_dram", a.shape, _mybir.dt.from_np(a.dtype), kind="ExternalInput").ap())
    for i, (shape, dtype) in enumerate(_OUTS):
        dt = _mybir.dt.from_np(_np.dtype(dtype))
        args.append(nc.dram_tensor(f"out_{i}_dram", shape, dt, kind="ExternalOutput").ap())
    gnn_kernel(nc, *args)
    r = _run(nc, [arrays], core_ids=[0])
    got = tuple(r.results[0][f"out_{i}_dram"] for i in range(len(_OUTS)))
    return got[0]
```
